# Optimizing a Trainium2 kernel written in Bass

```python
import numpy as np
import jax
import jax.numpy as jnp

def _softmax(x, axis=-1):
    return jax.nn.softmax(x, axis=axis)

def _gelu(x):
    return jax.nn.gelu(x, approximate=True)

def _silu(x):
    return jax.nn.silu(x)

def _sigmoid(x):
    return jax.nn.sigmoid(x)

def _layernorm(x, axis=-1, eps=1e-05):
    m = jnp.mean(x, axis=axis, keepdims=True)
    v = jnp.var(x, axis=axis, keepdims=True)
    return (x - m) / jnp.sqrt(v + eps)

def _scatter_add(tgt, idx, src, axis=0):
    return tgt.at[idx].add(src)

def _segment_sum(src, seg, n):
    return jax.ops.segment_sum(src, seg, n)
kernel_name = 'mk_xattn_seq_d2_seqx_r8_7fdb28'

def setup_inputs(seed: int=0):
    np.random.seed(seed)
    _w = jnp.asarray

    def _rec_inputs():
        import jax
        import jax.numpy as jnp
        _rk = jax.random.key(seed)
        x = 7.22e-05 + 1 * jax.random.normal(jax.random.fold_in(_rk, 1), (64, 64, 256), jnp.float32)
        _lenS = 64 - jax.random.randint(jax.random.fold_in(_rk, 7), (64,), 0, max(1, 64 // 4) + 1, jnp.int32)
        _lenS2 = 64 - jax.random.randint(jax.random.fold_in(_rk, 8), (64,), 0, max(1, 64 // 4) + 1, jnp.int32)
        _ctx_2048P = jax.random.normal(jax.random.fold_in(_rk, 11), (64, 16, 256), jnp.float32)
        _ctx_2048c = jax.random.dirichlet(jax.random.fold_in(_rk, 511), 0.3 * jnp.ones((16,), jnp.float32), (64, 64))
        _ctx_2048t = jnp.einsum('bsk,bkd->bsd', _ctx_2048c, _ctx_2048P)
        _ctx_2048t = _ctx_2048t * jax.lax.rsqrt(jnp.mean(jnp.square(_ctx_2048t)) + 1e-12) * 0.953939
        ctx_2048 = 4.13588e-05 + 0.999923 * (_ctx_2048t + 0.3 * jax.random.normal(jax.random.fold_in(_rk, 611), (64, 64, 256), jnp.float32))
        _validS = jnp.arange(64)[None, :] < _lenS[:, None]
        _validS2 = jnp.arange(64)[None, :] < _lenS2[:, None]
        _causal = jnp.tril(jnp.ones((64, 64), dtype=bool))
        mask_Bx1xSxS2_ff0 = jnp.where(jnp.ones((64, 1, 64, 64), dtype=bool), 0.0, -1000000000.0).astype(jnp.float32)
        return (x, ctx_2048, mask_Bx1xSxS2_ff0)
    x, ctx_2048, mask_Bx1xSxS2_ff0 = _rec_inputs()

    def _L0_xattn_setup():
        import jax, jax.numpy as jnp
        import numpy as np
        H = 256
        NH = 32
        KVH = 8
        HD = H // NH
        GROUPS = NH // KVH
        EPS = 1e-06
        B, L, S = (4, 128, 128)

        def _gqa_forward(hidden_state, encoder_hidden_state, encoder_attention_mask, Wq, bq, Wk, bk, Wv, bv, Wo, bo, gamma, beta):
            b, l, _ = hidden_state.shape
            s = encoder_hidden_state.shape[1]
            q = hidden_state @ Wq + bq
            k = encoder_hidden_state @ Wk + bk
            v = encoder_hidden_state @ Wv + bv
            q = q.reshape(b, l, KVH, GROUPS, HD).transpose(0, 2, 3, 1, 4)
            k = k.reshape(b, s, KVH, HD).transpose(0, 2, 1, 3)
            v = v.reshape(b, s, KVH, HD).transpose(0, 2, 1, 3)
            scale = 1.0 / jnp.sqrt(jnp.asarray(HD, q.dtype))
            scores = jnp.einsum('bkgld,bksd->bkgls', q, k) * scale
            scores = scores + encoder_attention_mask[:, :, None, :, :]
            attn = jax.nn.softmax(scores, axis=-1)
            out = jnp.einsum('bkgls,bksd->bkgld', attn, v)
            out = out.transpose(0, 3, 1, 2, 4).reshape(b, l, H)
            out = out @ Wo + bo
            x = out + hidden_state
            mu = jnp.mean(x, axis=-1, keepdims=True)
            var = jnp.var(x, axis=-1, keepdims=True)
            return (x - mu) * jax.lax.rsqrt(var + EPS) * gamma + beta
        key = jax.random.key(seed)
        ks = jax.random.split(key, 12)
        sd = 0.02
        return {'hidden_state': jax.random.normal(ks[0], (B, L, H), jnp.float32), 'encoder_hidden_state': jax.random.normal(ks[1], (B, S, H), jnp.float32), 'encoder_attention_mask': jnp.zeros((B, 1, L, S), jnp.float32), 'Wq': jax.random.normal(ks[2], (H, H), jnp.float32) * sd, 'bq': jnp.zeros((H,), jnp.float32), 'Wk': jax.random.normal(ks[3], (H, KVH * HD), jnp.float32) * sd, 'bk': jnp.zeros((KVH * HD,), jnp.float32), 'Wv': jax.random.normal(ks[4], (H, KVH * HD), jnp.float32) * sd, 'bv': jnp.zeros((KVH * HD,), jnp.float32), 'Wo': jax.random.normal(ks[5], (H, H), jnp.float32) * sd, 'bo': jnp.zeros((H,), jnp.float32), 'gamma': jnp.ones((H,), jnp.float32), 'beta': jnp.zeros((H,), jnp.float32)}
    _L0_xattn_all = _L0_xattn_setup()
    _L0_xattn_in = {k: v for k, v in _L0_xattn_all.items() if k in ('Wq', 'bq', 'Wk', 'bk', 'Wv', 'bv', 'Wo', 'bo', 'gamma', 'beta')}
    del _L0_xattn_all

    def _L1_xattn_setup():
        import jax, jax.numpy as jnp
        import numpy as np
        B, L, E, H = (4, 64, 256, 32)
        S = E // H
        EXTRA_MAA, EXTRA_DECAY = (32, 64)
        EPS = 1e-05

        def _ln(x, w, b):
            m = jnp.mean(x, axis=-1, keepdims=True)
            v = jnp.mean((x - m) ** 2, axis=-1, keepdims=True)
            return (x - m) * jax.lax.rsqrt(v + EPS) * w + b

        def _token_shift(xn, prev_row):
            first = (prev_row - xn[:, 0])[:, None]
            rest = xn[:, :-1] - xn[:, 1:]
            return jnp.concatenate([first, rest], axis=1)
        key = jax.random.key(seed)
        ks = jax.random.split(key, 24)
        rn = lambda k, shp, s=1.0: jax.random.normal(k, shp, dtype=jnp.float32) * s
        return dict(x=rn(ks[0], (B, L, E)), state=rn(ks[1], (B, 2 + S, E), 0.1), ln1_w=jnp.ones((E,), jnp.float32), ln1_b=jnp.zeros((E,), jnp.float32), ln2_w=jnp.ones((E,), jnp.float32), ln2_b=jnp.zeros((E,), jnp.float32), maa_x=rn(ks[2], (E,), 0.02), maa_w1=rn(ks[3], (E, 5 * EXTRA_MAA), 0.02), maa_w2=rn(ks[4], (5, EXTRA_MAA, E), 0.02), maa_stack=rn(ks[5], (5, E), 0.02), time_decay=rn(ks[6], (E,), 0.5), decay_w1=rn(ks[7], (E, EXTRA_DECAY), 0.02), decay_w2=rn(ks[8], (EXTRA_DECAY, E), 0.02), faaaa=rn(ks[9], (H, S), 0.1), Wr=rn(ks[10], (E, E), 0.02), Wk=rn(ks[11], (E, E), 0.02), Wv=rn(ks[12], (E, E), 0.02), Wg=rn(ks[13], (E, E), 0.02), Wo=rn(ks[14], (E, E), 0.02), gn_w=jnp.ones((E,), jnp.float32), gn_b=jnp.zeros((E,), jnp.float32), ffn_maa_k=rn(ks[15], (E,), 0.02), ffn_maa_r=rn(ks[16], (E,), 0.02), ffn_Wk=rn(ks[17], (E, E), 0.02), ffn_Wr=rn(ks[18], (E, E), 0.02), ffn_Wv=rn(ks[19], (E, E), 0.02), i=0)
    _L1_xattn_all = _L1_xattn_setup()
    _L1_xattn_in = {k: v for k, v in _L1_xattn_all.items() if k in ('ln1_w', 'ln1_b', 'ln2_w', 'ln2_b', 'maa_x', 'maa_w1', 'maa_w2', 'maa_stack', 'time_decay', 'decay_w1', 'decay_w2', 'faaaa', 'Wr', 'Wk', 'Wv', 'Wg', 'Wo', 'gn_w', 'gn_b', 'ffn_maa_k', 'ffn_maa_r', 'ffn_Wk', 'ffn_Wr', 'ffn_Wv')}
    del _L1_xattn_all
    return {'x': x, 'ctx_2048': ctx_2048, 'mask_Bx1xSxS2_ff0': mask_Bx1xSxS2_ff0, 'L0_xattn_Wq': _L0_xattn_in['Wq'], 'L0_xattn_bq': _L0_xattn_in['bq'], 'L0_xattn_Wk': _L0_xattn_in['Wk'], 'L0_xattn_bk': _L0_xattn_in['bk'], 'L0_xattn_Wv': _L0_xattn_in['Wv'], 'L0_xattn_bv': _L0_xattn_in['bv'], 'L0_xattn_Wo': _L0_xattn_in['Wo'], 'L0_xattn_bo': _L0_xattn_in['bo'], 'L0_xattn_gamma': _L0_xattn_in['gamma'], 'L0_xattn_beta': _L0_xattn_in['beta'], 'L1_xattn_ln1_w': _L1_xattn_in['ln1_w'], 'L1_xattn_ln1_b': _L1_xattn_in['ln1_b'], 'L1_xattn_ln2_w': _L1_xattn_in['ln2_w'], 'L1_xattn_ln2_b': _L1_xattn_in['ln2_b'], 'L1_xattn_maa_x': _L1_xattn_in['maa_x'], 'L1_xattn_maa_w1': _L1_xattn_in['maa_w1'], 'L1_xattn_maa_w2': _L1_xattn_in['maa_w2'], 'L1_xattn_maa_stack': _L1_xattn_in['maa_stack'], 'L1_xattn_time_decay': _L1_xattn_in['time_decay'], 'L1_xattn_decay_w1': _L1_xattn_in['decay_w1'], 'L1_xattn_decay_w2': _L1_xattn_in['decay_w2'], 'L1_xattn_faaaa': _L1_xattn_in['faaaa'], 'L1_xattn_Wr': _L1_xattn_in['Wr'], 'L1_xattn_Wk': _L1_xattn_in['Wk'], 'L1_xattn_Wv': _L1_xattn_in['Wv'], 'L1_xattn_Wg': _L1_xattn_in['Wg'], 'L1_xattn_Wo': _L1_xattn_in['Wo'], 'L1_xattn_gn_w': _L1_xattn_in['gn_w'], 'L1_xattn_gn_b': _L1_xattn_in['gn_b'], 'L1_xattn_ffn_maa_k': _L1_xattn_in['ffn_maa_k'], 'L1_xattn_ffn_maa_r': _L1_xattn_in['ffn_maa_r'], 'L1_xattn_ffn_Wk': _L1_xattn_in['ffn_Wk'], 'L1_xattn_ffn_Wr': _L1_xattn_in['ffn_Wr'], 'L1_xattn_ffn_Wv': _L1_xattn_in['ffn_Wv']}

def reference(x, ctx_2048, mask_Bx1xSxS2_ff0, L0_xattn_Wq, L0_xattn_bq, L0_xattn_Wk, L0_xattn_bk, L0_xattn_Wv, L0_xattn_bv, L0_xattn_Wo, L0_xattn_bo, L0_xattn_gamma, L0_xattn_beta, L1_xattn_ln1_w, L1_xattn_ln1_b, L1_xattn_ln2_w, L1_xattn_ln2_b, L1_xattn_maa_x, L1_xattn_maa_w1, L1_xattn_maa_w2, L1_xattn_maa_stack, L1_xattn_time_decay, L1_xattn_decay_w1, L1_xattn_decay_w2, L1_xattn_faaaa, L1_xattn_Wr, L1_xattn_Wk, L1_xattn_Wv, L1_xattn_Wg, L1_xattn_Wo, L1_xattn_gn_w, L1_xattn_gn_b, L1_xattn_ffn_maa_k, L1_xattn_ffn_maa_r, L1_xattn_ffn_Wk, L1_xattn_ffn_Wr, L1_xattn_ffn_Wv):
    import jax
    import jax.numpy as jnp

    def _L0_xattn_ref(hidden_state, encoder_hidden_state, encoder_attention_mask, Wq, bq, Wk, bk, Wv, bv, Wo, bo, gamma, beta):
        import jax, jax.numpy as jnp
        import numpy as np
        H = 256
        NH = 32
        KVH = 8
        HD = H // NH
        GROUPS = NH // KVH
        EPS = 1e-06
        B, L, S = (4, 128, 128)

        def _gqa_forward(hidden_state, encoder_hidden_state, encoder_attention_mask, Wq, bq, Wk, bk, Wv, bv, Wo, bo, gamma, beta):
            b, l, _ = hidden_state.shape
            s = encoder_hidden_state.shape[1]
            q = hidden_state @ Wq + bq
            k = encoder_hidden_state @ Wk + bk
            v = encoder_hidden_state @ Wv + bv
            q = q.reshape(b, l, KVH, GROUPS, HD).transpose(0, 2, 3, 1, 4)
            k = k.reshape(b, s, KVH, HD).transpose(0, 2, 1, 3)
            v = v.reshape(b, s, KVH, HD).transpose(0, 2, 1, 3)
            scale = 1.0 / jnp.sqrt(jnp.asarray(HD, q.dtype))
            scores = jnp.einsum('bkgld,bksd->bkgls', q, k) * scale
            scores = scores + encoder_attention_mask[:, :, None, :, :]
            attn = jax.nn.softmax(scores, axis=-1)
            out = jnp.einsum('bkgls,bksd->bkgld', attn, v)
            out = out.transpose(0, 3, 1, 2, 4).reshape(b, l, H)
            out = out @ Wo + bo
            x = out + hidden_state
            mu = jnp.mean(x, axis=-1, keepdims=True)
            var = jnp.var(x, axis=-1, keepdims=True)
            return (x - mu) * jax.lax.rsqrt(var + EPS) * gamma + beta
        return _gqa_forward(hidden_state, encoder_hidden_state, encoder_attention_mask, Wq, bq, Wk, bk, Wv, bv, Wo, bo, gamma, beta)

    def _L1_xattn_ref(x, state, ln1_w, ln1_b, ln2_w, ln2_b, maa_x, maa_w1, maa_w2, maa_stack, time_decay, decay_w1, decay_w2, faaaa, Wr, Wk, Wv, Wg, Wo, gn_w, gn_b, ffn_maa_k, ffn_maa_r, ffn_Wk, ffn_Wr, ffn_Wv, i):
        import jax, jax.numpy as jnp
        import numpy as np
        B, L, E, H = (4, 64, 256, 32)
        S = E // H
        EXTRA_MAA, EXTRA_DECAY = (32, 64)
        EPS = 1e-05

        def _ln(x, w, b):
            m = jnp.mean(x, axis=-1, keepdims=True)
            v = jnp.mean((x - m) ** 2, axis=-1, keepdims=True)
            return (x - m) * jax.lax.rsqrt(v + EPS) * w + b

        def _token_shift(xn, prev_row):
            first = (prev_row - xn[:, 0])[:, None]
            rest = xn[:, :-1] - xn[:, 1:]
            return jnp.concatenate([first, rest], axis=1)
        b, l = (x.shape[0], x.shape[1])
        i0 = (2 + S) * i + 0
        i1 = (2 + S) * i + 1
        xn = _ln(x, ln1_w, ln1_b)
        sx = _token_shift(xn, state[:, i1])
        xxx = jnp.tanh((xn + sx * maa_x) @ maa_w1).reshape(b, l, 5, 1, EXTRA_MAA)
        xxx = jnp.matmul(xxx, maa_w2).reshape(b, l, 5, E)
        x5 = xn[:, :, None] + sx[:, :, None] * (maa_stack + xxx)
        w = jnp.exp(-jnp.exp(time_decay + jnp.tanh(x5[:, :, 1] @ decay_w1) @ decay_w2))
        w = w.reshape(b, l, H, S)
        r = (x5[:, :, 3] @ Wr.T).reshape(b, l, H, S)
        k = (x5[:, :, 0] @ Wk.T).reshape(b, l, H, S)
        v = (x5[:, :, 2] @ Wv.T).reshape(b, l, H, S)
        g = jax.nn.silu(x5[:, :, 4] @ Wg.T)
        s0 = state[:, (2 + S) * i + 2:(2 + S) * (i + 1)].reshape(b, H, S, S)
        u = faaaa[None, :, :, None]

        def step(s, rkvw):
            r_t, k_t, v_t, w_t = rkvw
            a = k_t[:, :, :, None] * v_t[:, :, None, :]
            out = jnp.einsum('bhk,bhkd->bhd', r_t, u * a + s)
            return (a + w_t[:, :, :, None] * s, out)
        xs = tuple((jnp.moveaxis(t, 1, 0) for t in (r, k, v, w)))
        _, outs = jax.lax.scan(step, s0, xs)
        att = jnp.moveaxis(outs, 0, 1).reshape(b, l, E)
        a4 = att.reshape(b, l, H, S)
        m = jnp.mean(a4, axis=-1, keepdims=True)
        var = jnp.mean((a4 - m) ** 2, axis=-1, keepdims=True)
        att = ((a4 - m) * jax.lax.rsqrt(var + EPS)).reshape(b, l, E) * gn_w + gn_b
        x = x + att * g @ Wo.T
        xn2 = _ln(x, ln2_w, ln2_b)
        sx2 = _token_shift(xn2, state[:, i0])
        xk = xn2 + sx2 * ffn_maa_k
        xr = xn2 + sx2 * ffn_maa_r
        rr = jax.nn.sigmoid(xr @ ffn_Wr.T)
        kk = jnp.square(jax.nn.relu(xk @ ffn_Wk.T))
        x = x + rr * (kk @ ffn_Wv.T)
        return x
    x = _L0_xattn_ref(x, ctx_2048, mask_Bx1xSxS2_ff0, L0_xattn_Wq, L0_xattn_bq, L0_xattn_Wk, L0_xattn_bk, L0_xattn_Wv, L0_xattn_bv, L0_xattn_Wo, L0_xattn_bo, L0_xattn_gamma, L0_xattn_beta)
    x = _L1_xattn_ref(x, ctx_2048, L1_xattn_ln1_w, L1_xattn_ln1_b, L1_xattn_ln2_w, L1_xattn_ln2_b, L1_xattn_maa_x, L1_xattn_maa_w1, L1_xattn_maa_w2, L1_xattn_maa_stack, L1_xattn_time_decay, L1_xattn_decay_w1, L1_xattn_decay_w2, L1_xattn_faaaa, L1_xattn_Wr, L1_xattn_Wk, L1_xattn_Wv, L1_xattn_Wg, L1_xattn_Wo, L1_xattn_gn_w, L1_xattn_gn_b, L1_xattn_ffn_maa_k, L1_xattn_ffn_maa_r, L1_xattn_ffn_Wk, L1_xattn_ffn_Wr, L1_xattn_ffn_Wv, 0)
    return x

_drawn_inputs = setup_inputs


def setup_inputs(seed=0):
    import zlib

    import numpy as np

    out = dict(_drawn_inputs(seed))
    spreads = {'L0_xattn_bq': (0.0, 0.8),
     'L0_xattn_bk': (0.0, 0.8),
     'L0_xattn_bv': (0.0, 0.1),
     'L0_xattn_bo': (0.0, 0.1),
     'L0_xattn_gamma': (1.0, 0.2),
     'L0_xattn_beta': (0.0, 0.1),
     'L1_xattn_ln1_w': (1.0, 0.6),
     'L1_xattn_ln1_b': (0.0, 0.589),
     'L1_xattn_ln2_w': (1.0, 0.6),
     'L1_xattn_ln2_b': (0.0, 0.8),
     'L1_xattn_gn_w': (1.0, 0.6),
     'L1_xattn_gn_b': (0.0, 0.8)}
    factors = {'L0_xattn_Wq': 8.0,
     'L0_xattn_Wk': 8.0,
     'L1_xattn_maa_x': 8.0,
     'L1_xattn_maa_w1': 8.0,
     'L1_xattn_maa_w2': 8.0,
     'L1_xattn_maa_stack': 8.0,
     'L1_xattn_time_decay': 2.922,
     'L1_xattn_decay_w1': 8.0,
     'L1_xattn_decay_w2': 8.0,
     'L1_xattn_faaaa': 6.248,
     'L1_xattn_ffn_maa_k': 8.0,
     'L1_xattn_ffn_maa_r': 8.0,
     'L1_xattn_ffn_Wk': 2.992,
     'L1_xattn_ffn_Wr': 8.0,
     'L1_xattn_ffn_Wv': 2.778}
    for name, (base, spread) in spreads.items():
        noise = np.random.default_rng([zlib.crc32(name.encode()), seed]).standard_normal(out[name].shape)
        drawn = base * np.exp(spread * noise) if base else spread * noise
        out[name] = jnp.asarray(drawn.astype(out[name].dtype))
    for name, factor in factors.items():
        out[name] = (out[name] * factor).astype(out[name].dtype)
    return out
```

```python
from contextlib import ExitStack

import concourse.bass as bass
from concourse import mybir

P = 128
B, L, E = 64, 64, 256
NB = 4
STEPS = B // NB
TOK = NB * L
CM = 2 * TOK
KV, HD = 8, 8
QH = 32
HEADS_ROW = KV * L
SV = HD + 1
HS = 8
SCALE = float(1.0 / (HD ** 0.5))
EPS0, EPS1 = 1e-6, 1e-5

F32 = mybir.dt.float32
BF16 = mybir.dt.bfloat16
ALU = mybir.AluOpType
ACT = mybir.ActivationFunctionType
AXX = mybir.AxisListType.X

CONST = ["ident", "mean256", "sum8", "mean8", "center8"] + [f"rep{d}" for d in range(HS)] + \
        [f"red{d}" for d in range(HS)] + ["maskid"]
CONST_COLS = len(CONST) * P + KV
W0_COLS = {"wq": 512, "wk": 256, "wv": 128, "wo": 512, "bv": 64}
W1_COLS = {"w1": 320, "w2": 256, "w2b": 256, "dw1": 128, "dw2": 256, "wr": 512, "wkk": 512, "wvv": 512,
           "wg": 512, "woo": 512, "fr": 512, "fk": 512, "fv": 512}
VEC = ["bq", "bk", "bo", "gamma", "beta", "ln1w", "ln1b", "ln2w", "ln2b", "maax", "maa0", "maa1", "maa2",
       "maa3", "maa4", "td", "u", "gnw", "gnb", "fmk", "fmr"]
SEMS = ["c_in", "cdup", "x_in", "m_in", "st_in", "w_in", "ready",
        "k_mm", "v_mm", "q_mm", "k_ev", "v_ev", "q_ev", "kbd", "mask1", "mask2", "mask3", "mask4", "mask5",
        "qk_mm", "mx", "sub", "exp", "tr_mm", "pt_ev", "pv_mm", "rcp", "o_ev", "ot_mm", "ot_ev",
        "wo_mm", "u", "us", "mean0_mm", "d0", "sq0", "sqs0", "var0_mm", "ln0", "rstd0", "xh0", "x0",
        "st_used", "xs1", "mean1_mm", "d1", "sq1", "sqs1", "var1_mm", "ln1", "rstd1", "xh1", "xn1", "sx1",
        "z", "w1_mm", "xxx", "w2_mm", "mix", "x5", "dec1_mm", "dec1", "dec2_mm", "e", "w", "v1_mm", "v1",
        "k1_mm", "k1", "r1_mm", "r1", "g_mm", "gth", "gg", "ruk", "ruk_mm", "bonus", "vb_mm", "a", "s", "rs",
        "acc_mm", "sqg", "varg_mm", "lng", "rstdg", "xhg", "yg0", "yg", "wo1_mm", "x2",
        "xs2", "mean2_mm", "d2", "sq2", "sqs2", "var2_mm", "ln2", "rstd2", "xh2", "xn2", "sx2", "xr", "xk",
        "fr_mm", "rth", "fk_mm", "krelu", "kk", "fv_mm", "rk", "out", "out_st"]


def xattn_rwkv(nc, xT, cT, mask, st, consts, w0, w1, vec, outT):
    ctx = ExitStack()
    with ctx:
        def sb(name, cols, dt=F32):
            return ctx.enter_context(nc.sbuf_tensor(name, [P, cols], dt))

        S = {n: ctx.enter_context(nc.semaphore("s_" + n)) for n in SEMS}

        cst = sb("cst", CONST_COLS)
        C = {n: cst[:, k * P:(k + 1) * P] for k, n in enumerate(CONST)}
        bdmask = cst[:, len(CONST) * P:CONST_COLS]
        w0_sb = sb("w0_sb", sum(W0_COLS.values()))
        w1_sb = sb("w1_sb", sum(W1_COLS.values()))
        W = {}
        for tile, cols in ((w0_sb, W0_COLS), (w1_sb, W1_COLS)):
            at = 0
            for n, k in cols.items():
                W[n] = tile[:, at:at + k]
                at += k
        vec_sb = sb("vec_sb", 2 * len(VEC))

        def V(name, c):
            k = 2 * VEC.index(name) + c
            return vec_sb[:, k:k + 1]

        def Wc(name, c, lo=0, n=P):
            return W[name].rearrange("p (c n) -> p c n", c=2)[:, c, lo:lo + n]

        bqs = sb("bqs", 2)
        eps = sb("eps", 2)
        ones = sb("ones", 1)
        maskid = sb("maskid", P, BF16)

        x = sb("x", CM)
        c_ = sb("c_", CM)
        cdup = sb("cdup", 2 * CM)
        mraw = sb("mraw", TOK)
        mres = sb("mres", TOK)
        mmid = sb("mmid", TOK, BF16)
        mhm = sb("mhm", TOK, BF16)
        mlo = sb("mlo", TOK, BF16)
        q2 = sb("q2", 2 * NB * P)
        kT = sb("kT", TOK)
        kbd = sb("kbd", NB * HEADS_ROW)
        vbd = sb("vbd", NB * KV * SV)
        prob = [sb(f"prob{k}", 2 * HEADS_ROW) for k in range(2)]
        probT = [sb(f"probT{k}", 2 * HEADS_ROW) for k in range(2)]
        mx = sb("mx", 4 * KV)
        rcp = sb("rcp", 2 * KV)
        o = sb("o", P)
        oT = sb("oT", CM)
        u = sb("u", CM)
        us = sb("us", TOK)
        d0 = sb("d0", CM)
        sq0 = sb("sq0", CM)
        sqs0 = sb("sqs0", TOK)
        lnv0 = sb("lnv0", TOK)
        rstd0 = sb("rstd0", TOK)
        xh0 = sb("xh0", CM)
        x0 = sb("x0", CM)

        stt = sb("stt", 16 + 64)
        xs = sb("xs", TOK)
        d1 = sb("d1", CM)
        sq1 = sb("sq1", CM)
        sqs1 = sb("sqs1", TOK)
        lnv1 = sb("lnv1", CM)
        rstd1 = sb("rstd1", CM)
        xh1 = sb("xh1", CM)
        xn1 = sb("xn1", 2 * NB * (L + 1))
        xn2 = sb("xn2", 2 * NB * (L + 1))
        sx1 = sb("sx1", CM)
        sx2 = sb("sx2", CM)
        z = sb("z", CM)
        xxx = sb("xxx", CM)
        mix = [sb(f"mix{n}", CM) for n in range(5)]
        dec = sb("dec", TOK)
        e = sb("e", CM)
        wsh = sb("wsh", CM)
        v1 = sb("v1", CM)
        k1 = sb("k1", CM)
        r1 = sb("r1", CM)
        gth = sb("gth", CM)
        gg = sb("gg", CM)
        ruk = sb("ruk", CM)
        bonus = sb("bonus", CM)
        a_all = sb("a_all", HS * CM)
        state = [sb(f"state{n}", CM) for n in range(2)]
        rs = [sb(f"rs{n}", CM) for n in range(2)]
        yg = sb("yg", CM)
        x2 = sb("x2", CM)
        xk = sb("xk", CM)
        xr = sb("xr", CM)
        rth = sb("rth", CM)
        krelu = sb("krelu", CM)
        kk = sb("kk", CM)
        rk = sb("rk", CM)
        res = sb("res", CM)

        bank = [ctx.enter_context(nc.psum_tensor(f"bank{k}", [P, 512], F32)) for k in range(8)]
        SC = bank[0:2]
        TR = bank[2]
        M0 = bank[3]
        R = bank[4:7]
        ACC = bank[7]

        def two(ap):
            return ap.rearrange("p (c n) -> p c n", c=2)

        def both(ap):
            return ap.unsqueeze(1).broadcast_to([P, 2, TOK])

        def seqs(ap):
            return ap.rearrange("p (b t) -> p b t", b=2 * NB)

        def now(ap):
            return ap.rearrange("p (b t) -> p b t", b=2 * NB)[:, :, 1:L + 1]

        def before(ap):
            return ap.rearrange("p (b t) -> p b t", b=2 * NB)[:, :, 0:L]

        def half(ap, c):
            return two(ap)[:, c, :]

        def bt(ap):
            return ap.rearrange("p (b t) -> p b t", b=NB)

        def now_half(ap, c):
            return now(ap)[:, c * NB:(c + 1) * NB, :]

        def weights_ready(eng):
            eng.wait_ge(S["w_in"], 64)
            eng.wait_ge(S["ready"], 4)

        block = ctx.enter_context(nc.Block())

        @block.sync
        def _(sp):
            def load_attention(i, reuse=True):
                if reuse:
                    sp.wait_ge(S["v_mm"], i)
                sp.dma_start(c_[:, :], cT[bass.ds(i, 1), :, :].rearrange("a p n -> (a p) n")).then_inc(S["c_in"], 16)
                if reuse:
                    sp.wait_ge(S["mask5"], i)
                for h in range(2):
                    sp.dma_start(mraw[64 * h:64 * h + 64, :],
                                 mask[bass.ds(i, 1), :, :].rearrange("a p n -> (a p) n")).then_inc(S["m_in"], 16)
                if reuse:
                    sp.wait_ge(S["u"], 2 * i)
                sp.dma_start(x[:, :], xT[bass.ds(i, 1), :, :].rearrange("a p n -> (a p) n")).then_inc(S["x_in"], 16)

            def load_state(j, reuse=True):
                if reuse:
                    sp.wait_ge(S["st_used"], 3 * j)
                sp.dma_start(stt[:, :], st[bass.ds(j, 1), :, :].rearrange("a p n -> (a p) n")).then_inc(S["st_in"], 16)

            def store(j):
                sp.wait_ge(S["out"], j + 1)
                sp.dma_start(outT[bass.ds(j, 1), :, :].rearrange("a p n -> (a p) n"), res[:, :]).then_inc(S["out_st"], 16)

            sp.dma_start(w0_sb[:, :], w0).then_inc(S["w_in"], 16)
            sp.dma_start(vec_sb[:, :], vec).then_inc(S["w_in"], 16)
            load_attention(0, reuse=False)
            sp.dma_start(cst[:, :], consts).then_inc(S["w_in"], 16)
            sp.dma_start(w1_sb[:, :], w1).then_inc(S["w_in"], 16)
            load_state(0, reuse=False)
            load_attention(1)
            load_state(1)
            load_attention(2)
            store(0)
            with sp.Fori(2, STEPS - 1) as i:
                load_state(i)
                load_attention(i + 1)
                store(i - 1)
            load_state(STEPS - 1)
            store(STEPS - 2)
            store(STEPS - 1)
            sp.wait_ge(S["out_st"], 16 * STEPS)

        @block.tensor
        def _(pe):
            def mm(out, lhsT, rhs, start=True, stop=True):
                return nc.tensor.matmul(out, lhsT, rhs, start=start, stop=stop, skip_group_check=True)

            def dense(out, name, rhs, rows=P, lo=0, width=E):
                for m in range(2):
                    for c in range(2):
                        last = mm(two(out)[:, m, :], Wc(name, c, m * P), half(rhs, c), c == 0, c == 1)
                return last

            def kv_proj(i):
                pe.wait_ge(S["c_in"], 16 * (i + 1))
                pe.wait_ge(S["ln0"], i)
                for c in range(2):
                    last = mm(M0[:, 0:TOK], Wc("wk", c), half(c_[:, :], c), c == 0, c == 1)
                last.then_inc(S["k_mm"], 1)
                pe.wait_ge(S["cdup"], i + 1)
                pe.wait_ge(S["pt_ev"], 8 * i)
                for b in range(NB):
                    for c in range(2):
                        n = (c * NB + b) * P
                        last = mm(TR[:, b * 64:(b + 1) * 64], cdup[:, n:n + P],
                                  W["wv"].rearrange("p (c n) -> p c n", c=2)[:, c, :], c == 0, c == 1)
                last.then_inc(S["v_mm"], 1)

            def q_proj(i):
                pe.wait_ge(S["x_in"], 16 * (i + 1))
                pe.wait_ge(S["sub"], 8 * i)
                for gp in range(2):
                    for c in range(2):
                        last = mm(SC[gp][:, 0:TOK], Wc("wq", c, gp * P), half(x[:, :], c), c == 0, c == 1)
                    last.then_inc(S["q_mm"], 1)

            def qk(i, b):
                if b == 0:
                    pe.wait_ge(S["q_ev"], 4 * (i + 1))
                    pe.wait_ge(S["kbd"], i + 1)
                    pe.wait_ge(S["mask5"], i + 1)
                for gp in range(2):
                    if b > 0:
                        pe.wait_ge(S["sub"], 8 * i + 2 * (b - 1) + gp + 1)
                    n = (gp * NB + b) * P
                    mm(SC[gp][:, :], q2[:, n:n + P], kbd[:, b * HEADS_ROW:(b + 1) * HEADS_ROW], True, False)
                    for part in (mhm, mlo):
                        m = part[:, b * L:(b + 1) * L].unsqueeze(1).broadcast_to([P, KV, L])
                        last = mm(SC[gp][:, :].rearrange("p (k s) -> p k s", k=KV), maskid[:, :], m, False, part is mlo)
                    last.then_inc(S["qk_mm"], 1)

            def tr(i, b):
                for gp in range(2):
                    n = 8 * i + 2 * b + gp
                    pe.wait_ge(S["exp"], n + 1)
                    if b == 0 and gp == 0:
                        pe.wait_ge(S["v_ev"], 2 * (i + 1))
                    else:
                        pe.wait_ge(S["pt_ev"], n)
                    for p in range(4):
                        last = nc.tensor.transpose(TR[:, p * P:(p + 1) * P],
                                                   prob[b % 2][:, gp * HEADS_ROW + p * P:gp * HEADS_ROW + (p + 1) * P],
                                                   C["ident"])
                    last.then_inc(S["tr_mm"], 1)

            def pv(i, b):
                pe.wait_ge(S["pt_ev"], 8 * i + 2 * b + 2)
                if b == 0:
                    pe.wait_ge(S["k_ev"], i + 1)
                    pe.wait_ge(S["v_ev"], 2 * (i + 1))
                else:
                    pe.wait_ge(S["ot_ev"], 4 * i + b)
                for gp in range(2):
                    for p in range(4):
                        n = (gp * 4 + p) * 2 * SV
                        last = mm(M0[:, n:n + 2 * SV], probT[b % 2][:, gp * HEADS_ROW + p * P:gp * HEADS_ROW + (p + 1) * P],
                                  vbd[:, (b * 4 + p) * 2 * SV:(b * 4 + p + 1) * 2 * SV])
                last.then_inc(S["pv_mm"], 1)

            def otr(i, b):
                pe.wait_ge(S["o_ev"], 4 * i + b + 1)
                nc.tensor.transpose(M0[:, 256:256 + P], o[:, :], C["ident"]).then_inc(S["ot_mm"], 1)

            def wo(i):
                pe.wait_ge(S["ot_ev"], 4 * (i + 1))
                dense(M0[:, :], "wo", oT[:, :]).then_inc(S["wo_mm"], 1)

            def mean0(i):
                pe.wait_ge(S["us"], i + 1)
                mm(M0[:, 0:TOK], C["mean256"], us[:, :]).then_inc(S["mean0_mm"], 1)

            def var0(i):
                pe.wait_ge(S["sqs0"], i + 1)
                mm(M0[:, 0:TOK], C["mean256"], sqs0[:, :]).then_inc(S["var0_mm"], 1)

            def mean1(j):
                pe.wait_ge(S["xs1"], j + 1)
                pe.wait_ge(S["rth"], j)
                mm(R[0][:, 0:TOK], C["mean256"], xs[:, :]).then_inc(S["mean1_mm"], 1)

            def var1(j):
                pe.wait_ge(S["sqs1"], j + 1)
                pe.wait_ge(S["kk"], j)
                mm(R[1][:, 0:TOK], C["mean256"], sqs1[:, :]).then_inc(S["var1_mm"], 1)

            def w1mm(j):
                pe.wait_ge(S["z"], 2 * (j + 1))
                pe.wait_ge(S["rk"], j)
                for lo, n in ((0, P), (P, 32)):
                    for c in range(2):
                        last = mm(R[2][0:n, 2 * lo:2 * lo + TOK], Wc("w1", c, lo, n), half(z[:, :], c), c == 0, c == 1)
                last.then_inc(S["w1_mm"], 1)

            def w2mm(j, n, k):
                bk, free, count = [(R[0], "d1", 1), (R[1], "ln1", 1), (R[2], "xxx", 2), (R[1], "mix", 4), (R[1], "mix", 8)][k]
                if k == 0:
                    pe.wait_ge(S["xxx"], 2 * (j + 1))
                if k == 1:
                    pe.wait_ge(S["ln1"], j + 1)
                if k == 3:
                    pe.wait_ge(S["mix"], 10 * j + 4)
                if k == 4:
                    pe.wait_ge(S["mix"], 10 * j + 8)
                lhs = W["w2"][32 * n:32 * n + 32, :] if n < 4 else W["w2b"][0:32, :]
                rhs = xxx[32 * n:32 * n + 32, 0:TOK] if n < 4 else xxx[0:32, TOK:CM]
                for m in range(2):
                    last = mm(two(bk[:, :])[:, m, :], lhs[:, m * P:(m + 1) * P], rhs)
                last.then_inc(S["w2_mm"], 1)

            def dec1(j):
                pe.wait_ge(S["x5"], 5 * j + 1)
                for c in range(2):
                    last = mm(R[0][0:64, 0:TOK], Wc("dw1", c, 0, 64), half(mix[1][:, :], c), c == 0, c == 1)
                last.then_inc(S["dec1_mm"], 1)

            def v1mm(j):
                pe.wait_ge(S["x5"], 5 * j + 2)
                pe.wait_ge(S["mix"], 10 * j + 6)
                dense(R[2][:, :], "wvv", mix[2][:, :]).then_inc(S["v1_mm"], 1)

            def dec2(j):
                pe.wait_ge(S["dec1"], j + 1)
                for m in range(2):
                    last = mm(two(R[0][:, :])[:, m, :], W["dw2"][0:64, m * P:(m + 1) * P], dec[0:64, :])
                last.then_inc(S["dec2_mm"], 1)

            def k1mm(j):
                pe.wait_ge(S["x5"], 5 * j + 3)
                pe.wait_ge(S["v1"], j + 1)
                dense(R[2][:, :], "wkk", mix[0][:, :]).then_inc(S["k1_mm"], 1)

            def r1mm(j):
                pe.wait_ge(S["x5"], 5 * j + 4)
                pe.wait_ge(S["e"], 2 * (j + 1))
                dense(R[0][:, :], "wr", mix[3][:, :]).then_inc(S["r1_mm"], 1)

            def gmm(j):
                pe.wait_ge(S["x5"], 5 * j + 5)
                dense(R[1][:, :], "wg", mix[4][:, :]).then_inc(S["g_mm"], 1)

            def rukmm(j):
                pe.wait_ge(S["ruk"], 2 * (j + 1))
                for m in range(2):
                    last = mm(two(R[2][:, :])[:, m, :], C["sum8"], half(ruk[:, :], m))
                last.then_inc(S["ruk_mm"], 1)

            def vb(j, d):
                free, n = [("r1", 1), ("gg", 1), ("bonus", 1)][d] if d < 3 else ("a", d - 2)
                pe.wait_ge(S[free], HS * j + n if d >= 3 else j + n)
                for m in range(2):
                    last = mm(two(R[d % 3][:, :])[:, m, :], C[f"rep{d}"], half(v1[:, :], m))
                last.then_inc(S["vb_mm"], 1)

            def acc_bonus(j):
                pe.wait_ge(S["bonus"], j + 1)
                pe.wait_ge(S["xhg"], j)
                for m in range(2):
                    mm(two(ACC[:, :])[:, m, :], C["center8"], half(bonus[:, :], m), m == 0, False)

            def acc(j, d):
                pe.wait_ge(S["rs"], HS * j + d + 1)
                for m in range(2):
                    last = mm(two(ACC[:, :])[:, m, :], C[f"red{d}"], half(rs[d % 2][:, :], m), False, d == HS - 1)
                last.then_inc(S["acc_mm"], 1)

            def varg(j):
                pe.wait_ge(S["sqg"], j + 1)
                for m in range(2):
                    last = mm(two(R[2][:, :])[:, m, :], C["mean8"], half(sq1[:, :], m))
                last.then_inc(S["varg_mm"], 1)

            def wo1(j):
                pe.wait_ge(S["yg"], j + 1)
                dense(R[0][:, :], "woo", yg[:, :]).then_inc(S["wo1_mm"], 1)

            def mean2(j):
                pe.wait_ge(S["xs2"], j + 1)
                mm(R[1][:, 0:TOK], C["mean256"], xs[:, :]).then_inc(S["mean2_mm"], 1)

            def var2(j):
                pe.wait_ge(S["sqs2"], j + 1)
                mm(R[2][:, 0:TOK], C["mean256"], sqs1[:, :]).then_inc(S["var2_mm"], 1)

            def frmm(j):
                pe.wait_ge(S["xr"], 2 * (j + 1))
                dense(R[0][:, :], "fr", xr[:, :]).then_inc(S["fr_mm"], 1)

            def fkmm(j):
                pe.wait_ge(S["xk"], 2 * (j + 1))
                dense(R[1][:, :], "fk", xk[:, :]).then_inc(S["fk_mm"], 1)

            def fvmm(j):
                pe.wait_ge(S["kk"], j + 1)
                dense(R[2][:, :], "fv", kk[:, :]).then_inc(S["fv_mm"], 1)

            def step(i, j):
                A = i is not None
                Z = j is not None
                if A:
                    kv_proj(i)
                if Z:
                    mean1(j)
                if A:
                    q_proj(i)
                if Z:
                    var1(j)
                if A:
                    qk(i, 0)
                if Z:
                    w1mm(j)
                if A:
                    tr(i, 0)
                    qk(i, 1)
                if Z:
                    w2mm(j, 1, 0)
                    w2mm(j, 2, 1)
                    w2mm(j, 0, 2)
                    dec1(j)
                if A:
                    pv(i, 0)
                    tr(i, 1)
                if Z:
                    w2mm(j, 3, 3)
                    v1mm(j)
                    dec2(j)
                    w2mm(j, 4, 4)
                if A:
                    otr(i, 0)
                    qk(i, 2)
                if Z:
                    k1mm(j)
                    r1mm(j)
                    gmm(j)
                if A:
                    pv(i, 1)
                if Z:
                    vb(j, 0)
                    rukmm(j)
                    vb(j, 1)
                if A:
                    otr(i, 1)
                    tr(i, 2)
                if Z:
                    vb(j, 2)
                    acc_bonus(j)
                    acc(j, 0)
                    vb(j, 3)
                    acc(j, 1)
                if A:
                    pv(i, 2)
                    qk(i, 3)
                if Z:
                    vb(j, 4)
                    acc(j, 2)
                    vb(j, 5)
                    acc(j, 3)
                if A:
                    otr(i, 2)
                    tr(i, 3)
                if Z:
                    vb(j, 6)
                    acc(j, 4)
                    vb(j, 7)
                    acc(j, 5)
                if A:
                    pv(i, 3)
                if Z:
                    acc(j, 6)
                    acc(j, 7)
                if A:
                    otr(i, 3)
                if Z:
                    varg(j)
                if A:
                    wo(i)
                if Z:
                    wo1(j)
                if A:
                    mean0(i)
                if Z:
                    mean2(j)
                if A:
                    var0(i)
                if Z:
                    var2(j)
                    frmm(j)
                    fkmm(j)
                    fvmm(j)

            weights_ready(pe)
            step(0, None)
            step(1, 0)
            with pe.Fori(2, STEPS) as i:
                step(i, i - 1)
            step(None, STEPS - 1)

        @block.vector
        def _(dve):
            v = nc.vector

            def k_ev(i):
                dve.wait_ge(S["k_mm"], i + 1)
                dve.wait_ge(S["kbd"], i)
                v.tensor_scalar(kT[:, :], M0[:, 0:TOK], V("bk", 0), None, ALU.add).then_inc(S["k_ev"], 1)

            def v_ev(i):
                dve.wait_ge(S["v_mm"], i + 1)
                for h in range(2):
                    rows = slice(64 * h, 64 * h + 64)
                    src = TR[rows, 0:NB * 64].rearrange("p (b k d) -> p b k d", b=NB, k=KV)[:, :, h::2, :]
                    dst = vbd[rows, :].rearrange("p (b k d) -> p b k d", b=NB, k=KV)[:, :, h::2, 0:HD]
                    bias = W["bv"][rows, :].rearrange("p (k d) -> p k d", k=KV)[:, h::2, :]\
                        .unsqueeze(1).broadcast_to([64, NB, KV // 2, HD])
                    v.tensor_tensor(dst, src, bias, ALU.add).then_inc(S["v_ev"], 1)

            def softmax(i, b):
                for gp in range(2):
                    n = 8 * i + 2 * b + gp
                    sc = SC[gp][:, :].rearrange("p (k s) -> p k s", k=KV)
                    m = mx[:, (2 * (b % 2) + gp) * KV:(2 * (b % 2) + gp + 1) * KV]
                    dve.wait_ge(S["qk_mm"], n + 1)
                    v.tensor_reduce(m, sc, AXX, ALU.max).then_inc(S["mx"], 1)
                    dve.wait_ge(S["mx"], n + 1)
                    if b >= 2:
                        dve.wait_ge(S["tr_mm"], n - 3)
                    v.tensor_tensor(prob[b % 2][:, gp * HEADS_ROW:(gp + 1) * HEADS_ROW]
                                    .rearrange("p (k s) -> p k s", k=KV), sc,
                                    m.unsqueeze(2).broadcast_to([P, KV, L]), ALU.subtract).then_inc(S["sub"], 1)

            def o_ev(i, b):
                n = 4 * i + b + 1
                pvv = M0[:, 0:2 * KV * SV].rearrange("p (k d) -> p k d", d=SV)
                dve.wait_ge(S["pv_mm"], n)
                v.reciprocal(rcp[:, :], pvv[:, :, HD:SV].rearrange("p k d -> p (k d)")).then_inc(S["rcp"], 1)
                dve.wait_ge(S["rcp"], n)
                dve.wait_ge(S["ot_mm"], n - 1)
                v.tensor_tensor(o[:, :].rearrange("p (k d) -> p k d", d=HD), pvv[:, :, 0:HD],
                                rcp[:, :].unsqueeze(2).broadcast_to([P, 2 * KV, HD]), ALU.mult).then_inc(S["o_ev"], 1)

            def residual0(i):
                dve.wait_ge(S["wo_mm"], i + 1)
                for c in range(2):
                    v.scalar_tensor_tensor(half(u[:, :], c), half(M0[:, :], c), V("bo", c), half(x[:, :], c),
                                           ALU.add, ALU.add).then_inc(S["u"], 1)

            def center(n, mean_sem, bk, src, dst, done):
                dve.wait_ge(S[mean_sem], n + 1)
                v.tensor_tensor(two(dst[:, :]), two(src[:, :]), both(bk[:, 0:TOK]), ALU.subtract).then_inc(S[done], 1)

            def normal(n, rstd_sem, src, rstd, dst, done):
                dve.wait_ge(S[rstd_sem], n + 1)
                v.tensor_tensor(two(dst[:, :]), two(src[:, :]), both(rstd[:, 0:TOK]), ALU.mult).then_inc(S[done], 1)

            def mixin(n, xn, sx, name, dst, done):
                for c in range(2):
                    v.scalar_tensor_tensor(bt(half(dst[:, :], c)), bt(half(sx[:, :], c)), V(name, c), now_half(xn, c),
                                           ALU.mult, ALU.add).then_inc(S[done], 1)

            def zmix(j):
                dve.wait_ge(S["sx1"], j + 1)
                mixin(j, xn1[:, :], sx1, "maax", z, "z")

            def mixes(j, n, k):
                dve.wait_ge(S["w2_mm"], 5 * j + k + 1)
                bk = [R[0], R[1], R[2], R[1], R[1]][k]
                for c in range(2):
                    v.scalar_tensor_tensor(half(mix[n][:, :], c), half(bk[:, :], c), V(f"maa{n}", c), half(sx1[:, :], c),
                                           ALU.add, ALU.mult).then_inc(S["mix"], 1)

            def ggate(j):
                dve.wait_ge(S["gth"], j + 1)
                v.scalar_tensor_tensor(gg[:, :], gth[:, :], 1.0, R[1][:, :], ALU.add, ALU.mult).then_inc(S["gg"], 1)

            def rukf(j):
                dve.wait_ge(S["r1"], j + 1)
                for c in range(2):
                    v.scalar_tensor_tensor(half(ruk[:, :], c), half(k1[:, :], c), V("u", c), half(r1[:, :], c),
                                           ALU.mult, ALU.mult).then_inc(S["ruk"], 1)

            def bonusf(j):
                dve.wait_ge(S["ruk_mm"], j + 1)
                v.tensor_tensor(bonus[:, :], R[2][:, :], v1[:, :], ALU.mult).then_inc(S["bonus"], 1)

            def outer(j, d):
                n = HS * j + d + 1
                dve.wait_ge(S["vb_mm"], n)
                a = a_all[:, d * CM:(d + 1) * CM]
                if d == 0:
                    dve.wait_ge(S["st_used"], 3 * (j + 1))
                    dve.wait_ge(S["w"], j + 1)
                v.tensor_tensor(seqs(a)[:, :, 1:L], seqs(k1[:, :])[:, :, 0:L - 1], seqs(R[d % 3][:, :])[:, :, 0:L - 1],
                                ALU.mult).then_inc(S["a"], 1)

            def scan(j, d):
                n = HS * j + d + 1
                a = a_all[:, d * CM:(d + 1) * CM]
                dve.wait_ge(S["a"], n)
                if d >= 2:
                    dve.wait_ge(S["rs"], n - 2)
                v.tensor_tensor_scan(state[d % 2][:, :], wsh[:, :], a, 0.0, ALU.mult, ALU.add).then_inc(S["s"], 1)

            def receive(j, d):
                n = HS * j + d + 1
                dve.wait_ge(S["s"], n)
                if d >= 2:
                    dve.wait_ge(S["acc_mm"], n - 2)
                v.tensor_tensor(rs[d % 2][:, :], r1[:, :], state[d % 2][:, :], ALU.mult).then_inc(S["rs"], 1)

            def xhg(j):
                dve.wait_ge(S["rstdg"], j + 1)
                v.tensor_tensor(xh1[:, :], ACC[:, :], rstd1[:, :], ALU.mult).then_inc(S["xhg"], 1)

            def gate(j):
                dve.wait_ge(S["yg0"], 2 * (j + 1))
                v.tensor_tensor(yg[:, :], xh1[:, :], gg[:, :], ALU.mult).then_inc(S["yg"], 1)

            def res2(j):
                dve.wait_ge(S["wo1_mm"], j + 1)
                v.scalar_tensor_tensor(x2[:, :], R[0][:, :], 0.5, x0[:, :], ALU.mult, ALU.add).then_inc(S["x2"], 1)

            def ffn_mix(j):
                dve.wait_ge(S["sx2"], j + 1)
                mixin(j, xn2[:, :], sx2, "fmr", xr, "xr")
                mixin(j, xn2[:, :], sx2, "fmk", xk, "xk")

            def kkf(j):
                dve.wait_ge(S["krelu"], j + 1)
                v.tensor_tensor(kk[:, :], krelu[:, :], R[1][:, :], ALU.mult).then_inc(S["kk"], 1)

            def rkf(j):
                dve.wait_ge(S["fv_mm"], j + 1)
                v.scalar_tensor_tensor(rk[:, :], rth[:, :], 1.0, R[2][:, :], ALU.add, ALU.mult).then_inc(S["rk"], 1)

            def outf(j):
                dve.wait_ge(S["rk"], j + 1)
                dve.wait_ge(S["out_st"], 16 * j)
                v.scalar_tensor_tensor(res[:, :], rk[:, :], 0.5, x2[:, :], ALU.mult, ALU.add).then_inc(S["out"], 1)

            def step(i, j):
                A = i is not None
                Z = j is not None
                if A:
                    k_ev(i)
                    v_ev(i)
                if Z:
                    center(j, "mean1_mm", R[0], x0, d1, "d1")
                if A:
                    softmax(i, 0)
                if Z:
                    normal(j, "rstd1", d1, rstd1, xh1, "xh1")
                    zmix(j)
                if A:
                    softmax(i, 1)
                if Z:
                    mixes(j, 1, 0)
                    mixes(j, 2, 1)
                    mixes(j, 0, 2)
                if A:
                    o_ev(i, 0)
                if Z:
                    mixes(j, 3, 3)
                    mixes(j, 4, 4)
                if A:
                    softmax(i, 2)
                    o_ev(i, 1)
                if Z:
                    rukf(j)
                    ggate(j)
                    bonusf(j)
                    outer(j, 0)
                    scan(j, 0)
                    outer(j, 1)
                    receive(j, 0)
                    scan(j, 1)
                    outer(j, 2)
                    receive(j, 1)
                if A:
                    o_ev(i, 2)
                    softmax(i, 3)
                if Z:
                    for d in range(2, HS - 1):
                        scan(j, d)
                        outer(j, d + 1)
                        receive(j, d)
                if A:
                    o_ev(i, 3)
                if Z:
                    scan(j, HS - 1)
                    receive(j, HS - 1)
                if A:
                    residual0(i)
                if Z:
                    xhg(j)
                    gate(j)
                if A:
                    center(i, "mean0_mm", M0, u, d0, "d0")
                if Z:
                    res2(j)
                    center(j, "mean2_mm", R[1], x2, d1, "d2")
                if A:
                    normal(i, "rstd0", d0, rstd0, xh0, "xh0")
                if Z:
                    normal(j, "rstd2", d1, rstd1, xh1, "xh2")
                    ffn_mix(j)
                    kkf(j)
                    rkf(j)
                    outf(j)

            v.memset(q2[:, :], 0.0).then_inc(S["ready"], 1)
            v.memset(vbd[:, :], 0.0).then_inc(S["ready"], 1)
            v.memset(eps[:, 0:1], EPS0)
            v.memset(ones[:, :], 1.0)
            v.memset(eps[:, 1:2], EPS1)
            dve.wait_ge(S["w_in"], 64)
            v.tensor_scalar(bqs[:, :], vec_sb[:, 0:2], SCALE, None, ALU.mult)
            dve.wait_ge(S["ready"], 2)
            for h in range(2):
                rows = slice(64 * h, 64 * h + 64)
                last = v.memset(vbd[rows, :].rearrange("p (b k d) -> p b k d", b=NB, k=KV)[:, :, h::2, HD:SV], 1.0)
            last.then_inc(S["ready"], 1)
            v.memset(seqs(wsh[:, :])[:, :, 0:1], 0.0)
            v.memset(mlo[64:P, :], 0.0)
            v.tensor_copy(maskid[:, :], C["maskid"]).then_inc(S["ready"], 1)
            weights_ready(dve)
            step(0, None)
            step(1, 0)
            with dve.Fori(2, STEPS) as i:
                step(i, i - 1)
            step(None, STEPS - 1)

        @block.scalar
        def _(act):
            s = nc.scalar

            def q_ev(i):
                for gp in range(2):
                    act.wait_ge(S["q_mm"], 2 * i + gp + 1)
                    for h in range(2):
                        rows = slice(64 * h, 64 * h + 64)
                        dst = q2[rows, :].rearrange("p (g b h t) -> p g b h t", g=2, b=NB, h=2)[:, gp, :, h, :]
                        s.activation(dst, bt(SC[gp][rows, 0:TOK]), ACT.Identity, bias=bqs[rows, gp:gp + 1],
                                     scale=SCALE).then_inc(S["q_ev"], 1)

            def expo(i, b):
                for gp in range(2):
                    act.wait_ge(S["sub"], 8 * i + 2 * b + gp + 1)
                    p = prob[b % 2][:, gp * HEADS_ROW:(gp + 1) * HEADS_ROW]
                    s.activation(p, p, ACT.Exp).then_inc(S["exp"], 1)

            def pt_ev(i, b):
                for gp in range(2):
                    act.wait_ge(S["tr_mm"], 8 * i + 2 * b + gp + 1)
                    s.copy(probT[b % 2][:, gp * HEADS_ROW:(gp + 1) * HEADS_ROW], TR[:, :]).then_inc(S["pt_ev"], 1)

            def ot_ev(i, b):
                act.wait_ge(S["ot_mm"], 4 * i + b + 1)
                s.copy(oT[:, :].rearrange("p (h b t) -> p h b t", h=2, b=NB)[:, :, b, :],
                       M0[:, 256:256 + P].rearrange("p (h t) -> p h t", h=2)).then_inc(S["ot_ev"], 1)

            def square(n, after, src, dst, done):
                act.wait_ge(S[after], n + 1)
                s.activation(dst[:, :], src[:, :], ACT.Square).then_inc(S[done], 1)

            def rsqrt(n, after, bk, cols, k, lnv, rstd, ln_done, done):
                act.wait_ge(S[after], n + 1)
                s.activation(lnv[:, 0:cols], bk[:, 0:cols], ACT.Ln, bias=eps[:, k:k + 1]).then_inc(S[ln_done], 1)
                act.wait_ge(S[ln_done], n + 1)
                s.activation(rstd[:, 0:cols], lnv[:, 0:cols], ACT.Exp, scale=-0.5).then_inc(S[done], 1)

            def affine(src, dst_half, w, b, done):
                for c in range(2):
                    s.activation(dst_half(c), bt(half(src[:, :], c)), ACT.Identity, bias=V(b, c), scale=V(w, c))\
                        .then_inc(S[done], 1)

            def step(i, j):
                A = i is not None
                Z = j is not None
                if A:
                    q_ev(i)
                if Z:
                    square(j, "d1", d1, sq1, "sq1")
                if A:
                    expo(i, 0)
                if Z:
                    rsqrt(j, "var1_mm", R[1], TOK, 1, lnv1, rstd1, "ln1", "rstd1")
                    act.wait_ge(S["xh1"], j + 1)
                    affine(xh1, lambda c: now_half(xn1[:, :], c), "ln1w", "ln1b", "xn1")
                if A:
                    pt_ev(i, 0)
                    expo(i, 1)
                if Z:
                    act.wait_ge(S["w1_mm"], j + 1)
                    s.activation(xxx[:, 0:TOK], R[2][:, 0:TOK], ACT.Tanh).then_inc(S["xxx"], 1)
                    s.activation(xxx[0:32, TOK:CM], R[2][0:32, TOK:CM], ACT.Tanh).then_inc(S["xxx"], 1)
                    act.wait_ge(S["dec1_mm"], j + 1)
                    s.activation(dec[0:64, :], R[0][0:64, 0:TOK], ACT.Tanh).then_inc(S["dec1"], 1)
                if A:
                    pt_ev(i, 1)
                if Z:
                    act.wait_ge(S["v1_mm"], j + 1)
                    s.copy(v1[:, :], R[2][:, :]).then_inc(S["v1"], 1)
                    act.wait_ge(S["dec2_mm"], j + 1)
                    for c in range(2):
                        s.activation(half(e[:, :], c), half(R[0][:, :], c), ACT.Exp, bias=V("td", c)).then_inc(S["e"], 1)
                    act.wait_ge(S["e"], 2 * (j + 1))
                    s.activation(seqs(wsh[:, :])[:, :, 1:L], seqs(e[:, :])[:, :, 0:L - 1], ACT.Exp, scale=-1.0)\
                        .then_inc(S["w"], 1)
                if A:
                    ot_ev(i, 0)
                    expo(i, 2)
                if Z:
                    act.wait_ge(S["k1_mm"], j + 1)
                    s.copy(k1[:, :], R[2][:, :]).then_inc(S["k1"], 1)
                    act.wait_ge(S["r1_mm"], j + 1)
                    s.copy(r1[:, :], R[0][:, :]).then_inc(S["r1"], 1)
                    act.wait_ge(S["g_mm"], j + 1)
                    s.activation(gth[:, :], R[1][:, :], ACT.Tanh, scale=0.5).then_inc(S["gth"], 1)
                if A:
                    ot_ev(i, 1)
                    pt_ev(i, 2)
                    expo(i, 3)
                    ot_ev(i, 2)
                    pt_ev(i, 3)
                    ot_ev(i, 3)
                if Z:
                    act.wait_ge(S["acc_mm"], HS * (j + 1))
                    s.activation(sq1[:, :], ACC[:, :], ACT.Square).then_inc(S["sqg"], 1)
                    rsqrt(j, "varg_mm", R[2], CM, 1, lnv1, rstd1, "lng", "rstdg")
                    act.wait_ge(S["xhg"], j + 1)
                    for c in range(2):
                        s.activation(half(xh1[:, :], c), half(xh1[:, :], c), ACT.Identity, bias=V("gnb", c),
                                     scale=V("gnw", c)).then_inc(S["yg0"], 1)
                if A:
                    square(i, "d0", d0, sq0, "sq0")
                if Z:
                    square(j, "d2", d1, sq1, "sq2")
                if A:
                    rsqrt(i, "var0_mm", M0, TOK, 0, lnv0, rstd0, "ln0", "rstd0")
                if Z:
                    rsqrt(j, "var2_mm", R[2], TOK, 1, lnv1, rstd1, "ln2", "rstd2")
                if A:
                    act.wait_ge(S["xh0"], i + 1)
                    if Z:
                        act.wait_ge(S["x2"], j + 1)
                    affine(xh0, lambda c: bt(half(x0[:, :], c)), "gamma", "beta", "x0")
                if Z:
                    act.wait_ge(S["xh2"], j + 1)
                    affine(xh1, lambda c: now_half(xn2[:, :], c), "ln2w", "ln2b", "xn2")
                    act.wait_ge(S["fr_mm"], j + 1)
                    s.activation(rth[:, :], R[0][:, :], ACT.Tanh, scale=0.5).then_inc(S["rth"], 1)
                    act.wait_ge(S["fk_mm"], j + 1)
                    s.activation(krelu[:, :], R[1][:, :], ACT.Relu).then_inc(S["krelu"], 1)

            weights_ready(act)
            step(0, None)
            step(1, 0)
            with act.Fori(2, STEPS) as i:
                step(i, i - 1)
            step(None, STEPS - 1)

        @block.gpsimd
        def _(pool):
            g = nc.gpsimd

            def copy(dst, src, rows=slice(0, P)):
                one = ones[rows, :]
                for _ in range(len(src.shape) - 2):
                    one = one.unsqueeze(1)
                return g.tensor_tensor(dst, src, one.broadcast_to(src.shape), ALU.mult)

            def split_mask(i):
                pool.wait_ge(S["m_in"], 32 * (i + 1))
                pool.wait_ge(S["qk_mm"], 8 * i)
                copy(mhm[:, :], mraw[:, :]).then_inc(S["mask1"], 1)
                pool.wait_ge(S["mask1"], i + 1)
                g.tensor_tensor(mres[:, :], mraw[:, :], mhm[:, :], ALU.subtract).then_inc(S["mask2"], 1)
                pool.wait_ge(S["mask2"], i + 1)
                copy(mmid[:, :], mres[:, :]).then_inc(S["mask3"], 1)
                pool.wait_ge(S["mask3"], i + 1)
                copy(mhm[64:P, :], mmid[64:P, :], slice(64, P)).then_inc(S["mask4"], 1)
                g.tensor_tensor(mlo[0:64, :], mres[0:64, :], mmid[0:64, :], ALU.subtract).then_inc(S["mask5"], 1)

            def duplicate(i):
                pool.wait_ge(S["c_in"], 16 * (i + 1))
                pool.wait_ge(S["v_mm"], i)
                copy(cdup[:, :].rearrange("p (b h t) -> p b h t", b=2 * NB, h=2),
                              seqs(c_[:, :]).unsqueeze(2).broadcast_to([P, 2 * NB, 2, L])).then_inc(S["cdup"], 1)

            def kbdf(i):
                pool.wait_ge(S["k_ev"], i + 1)
                k4 = [P, NB, KV, L]
                g.tensor_tensor(kbd[:, :].rearrange("p (b k s) -> p b k s", b=NB, k=KV),
                                bt(kT[:, :]).unsqueeze(2).broadcast_to(k4),
                                bdmask.unsqueeze(1).unsqueeze(3).broadcast_to(k4), ALU.mult).then_inc(S["kbd"], 1)

            def fold(n, after, times, src, dst, done):
                pool.wait_ge(S[after], times * (n + 1))
                g.tensor_tensor(dst[:, :], half(src[:, :], 0), half(src[:, :], 1), ALU.add).then_inc(S[done], 1)

            def shift(j, after, xn, sx, done):
                pool.wait_ge(S[after], 2 * (j + 1))
                g.tensor_tensor(seqs(sx[:, :]), before(xn[:, :]), now(xn[:, :]), ALU.subtract).then_inc(S[done], 1)

            def states(j):
                pool.wait_ge(S["st_in"], 16 * (j + 1))
                pool.wait_ge(S["xk"], 2 * j)
                pool.wait_ge(S["s"], HS * j)
                for k, xn in enumerate((xn1, xn2)):
                    copy(xn[:, :].rearrange("p (b t) -> p b t", b=2 * NB)[:, :, 0:1],
                                  stt[:, 8 * k:8 * k + 8].unsqueeze(2)).then_inc(S["st_used"], 1)
                copy(a_all[:, :].rearrange("p (d t) -> p d t", t=L)[:, :, 0:1],
                              stt[:, 16:80].unsqueeze(2)).then_inc(S["st_used"], 1)

            def add5(j, n, k):
                pool.wait_ge(S["mix"], 10 * j + 2 * k + 2)
                g.tensor_tensor(seqs(mix[n][:, :]), seqs(mix[n][:, :]), now(xn1[:, :]), ALU.add).then_inc(S["x5"], 1)

            def step(i, j):
                A = i is not None
                Z = j is not None
                if Z:
                    fold(j, "x0", 2, x0, xs, "xs1")
                if A:
                    duplicate(i)
                    kbdf(i)
                if Z:
                    states(j)
                    fold(j, "sq1", 1, sq1, sqs1, "sqs1")
                if A:
                    split_mask(i)
                if Z:
                    shift(j, "xn1", xn1, sx1, "sx1")
                    for k, n in enumerate((1, 2, 0, 3, 4)):
                        add5(j, n, k)
                if A:
                    fold(i, "u", 2, u, us, "us")
                if Z:
                    fold(j, "x2", 1, x2, xs, "xs2")
                if A:
                    fold(i, "sq0", 1, sq0, sqs0, "sqs0")
                if Z:
                    fold(j, "sq2", 1, sq1, sqs1, "sqs2")
                    shift(j, "xn2", xn2, sx2, "sx2")

            weights_ready(pool)
            step(0, None)
            step(1, 0)
            with pool.Fori(2, STEPS) as i:
                step(i, i - 1)
            step(None, STEPS - 1)


def kernel(**inputs):
    import numpy as np
    import concourse.bacc as bacc
    from concourse.bass_utils import run_bass_kernel_spmd

    I = {k: np.asarray(v) for k, v in inputs.items()}
    L0 = {k[9:]: v for k, v in I.items() if k.startswith("L0_xattn_")}
    L1 = {k[9:]: v for k, v in I.items() if k.startswith("L1_xattn_")}

    def cm(a):
        return a.reshape(STEPS, TOK, 2, P).transpose(0, 3, 2, 1).reshape(STEPS, P, CM)

    def rows(w):
        return w.reshape(2, P, -1).transpose(1, 0, 2).reshape(P, -1)

    def pad(w):
        return np.concatenate([w, np.zeros((P - w.shape[0], w.shape[1]), w.dtype)])

    q_order = np.arange(E).reshape(KV, 2, 2, HD).transpose(1, 2, 0, 3).reshape(-1)
    o_order = np.arange(E).reshape(KV, 2, 2, HD).transpose(2, 1, 0, 3).reshape(-1)
    ctx = I["ctx_2048"]
    first = ctx[:, 0:2, :].reshape(STEPS, NB, 2, 2, P)[:, :, ::-1].transpose(0, 4, 2, 3, 1).reshape(STEPS, P, 16)
    s0 = ctx[:, 2:2 + HS, :].reshape(STEPS, NB, 2, P, HS).transpose(0, 3, 4, 2, 1).reshape(STEPS, P, 64)

    p = np.arange(P)
    same = (p[:, None] // HS == p[None, :] // HS).astype(np.float32)
    eye = np.eye(P, dtype=np.float32)
    table = {"ident": eye, "mean256": np.full((P, P), 1.0 / E, np.float32), "sum8": same, "mean8": same / HS,
             "center8": eye - same / HS, "maskid": (p[:, None] % L == p[None, :] % L).astype(np.float32)}
    for d in range(HS):
        table[f"rep{d}"] = same * (p[:, None] % HS == d)
        table[f"red{d}"] = same * ((p[None, :] % HS == d) - np.float32(1.0 / HS))
    bd = ((p[:, None] % 64) // HD == np.arange(KV)[None, :]).astype(np.float32)
    consts = np.concatenate([table[n].astype(np.float32) for n in CONST] + [bd], axis=1)

    w0 = {"wq": rows(L0["Wq"][:, q_order]), "wk": rows(np.concatenate([L0["Wk"]] * 2, 1)), "wv": rows(L0["Wv"]),
          "wo": rows(L0["Wo"][o_order]), "bv": np.repeat(L0["bv"][None], P, 0)}
    w1 = {"w1": rows(L1["maa_w1"]), "w2": L1["maa_w2"][:4].reshape(P, E), "w2b": pad(L1["maa_w2"][4]),
          "dw1": rows(L1["decay_w1"]), "dw2": pad(L1["decay_w2"]), "wr": rows(L1["Wr"].T), "wkk": rows(L1["Wk"].T),
          "wvv": rows(L1["Wv"].T), "wg": rows(L1["Wg"].T), "woo": rows(L1["Wo"].T), "fr": rows(L1["ffn_Wr"].T),
          "fk": rows(L1["ffn_Wk"].T), "fv": rows(L1["ffn_Wv"].T)}
    vecs = {"bq": L0["bq"][q_order], "bk": np.concatenate([L0["bk"]] * 4), "bo": L0["bo"], "gamma": L0["gamma"],
            "beta": L0["beta"], "ln1w": L1["ln1_w"], "ln1b": L1["ln1_b"], "ln2w": L1["ln2_w"], "ln2b": L1["ln2_b"],
            "maax": L1["maa_x"], "td": L1["time_decay"], "u": L1["faaaa"].reshape(-1), "gnw": L1["gn_w"],
            "gnb": L1["gn_b"], "fmk": L1["ffn_maa_k"], "fmr": L1["ffn_maa_r"]}
    for n in range(5):
        vecs[f"maa{n}"] = L1["maa_stack"][n]

    arrays = {
        "xT": cm(I["x"]), "cT": cm(ctx),
        "mask": I["mask_Bx1xSxS2_ff0"].reshape(STEPS, NB, L, L).transpose(0, 2, 1, 3).reshape(STEPS, L, NB * L),
        "st": np.concatenate([first, s0], axis=2),
        "consts": consts,
        "w0": np.concatenate([w0[n] for n in W0_COLS], axis=1),
        "w1": np.concatenate([w1[n] for n in W1_COLS], axis=1),
        "vec": np.concatenate([vecs[n].reshape(2, P).T for n in VEC], axis=1),
    }
    arrays = {k: np.ascontiguousarray(a) for k, a in arrays.items()}
    nc = bacc.Bacc("TRN2", target_bir_lowering=False, num_devices=1)
    args = [nc.dram_tensor(k, a.shape, F32, kind="ExternalInput").ap() for k, a in arrays.items()]
    out = nc.dram_tensor("out", (STEPS, P, CM), F32, kind="ExternalOutput").ap()
    xattn_rwkv(nc, *args, out)
    r = run_bass_kernel_spmd(nc, [arrays], core_ids=[0])
    y = r.results[0]["out"]
    return y.reshape(STEPS, P, 2, TOK).transpose(0, 3, 2, 1).reshape(B, L, E)
```

```python
from contextlib import ExitStack

import concourse.bass as bass
from concourse import mybir

P = 128
B, L, E = 64, 64, 256
NB = 4
STEPS = B // NB
TOK = NB * L
CM = 2 * TOK
KV, HD = 8, 8
GROUP = KV * L
SV = HD + 1
HS = 8
PAIRS = HS // 2
SCALE = float(1.0 / (HD ** 0.5))
EPS0, EPS1 = 1e-6, 1e-5
MIXES = (1, 2, 0, 3, 4)

F32 = mybir.dt.float32
BF16 = mybir.dt.bfloat16
ALU = mybir.AluOpType
ACT = mybir.ActivationFunctionType
AXX = mybir.AxisListType.X

CONST = ["ident", "mean256", "sum8", "mean8", "center8"] + [f"red{d}" for d in range(HS)] + ["maskid"]
CONST_COLS = len(CONST) * P + KV
W0_COLS = {"wq": 512, "wk": 256, "wv": 128, "wo": 512, "bv": 64}
W1_COLS = {"w1": 320, "w2": 256, "w2b": 256, "dw1": 128, "dw2": 256, "wr": 512, "wkk": 512, "wvv": 512,
           "wg": 512, "woo": 512, "fr": 512, "fk": 512, "fv": 512}
VEC = ["bq", "bk", "bo", "gamma", "beta", "ln1w", "ln1b", "ln2w", "ln2b", "maax", "maa0", "maa1", "maa2",
       "maa3", "maa4", "td", "u", "gnw", "gnb", "fmk", "fmr"]
FIRST, REST = 2 * NB, 2 * NB + 64
SEMS = [
    "w_in", "w1_in", "ready", "c_in", "xq_in", "x_in", "m_in", "first_in", "rest_in",
    "cdup", "k_mm", "k_ev", "kbd", "q_mm", "q_ev", "v_mm", "v_ev", "mask1", "mask2", "mask3", "mask4", "mask5",
    "qk_mm", "mx", "sub", "exp", "tr_mm", "pt_ev", "pv_mm", "rcp", "o_ev", "ot_mm", "ot_ev",
    "wo_mm", "u", "us", "mean0_mm", "d0", "sq0", "sqs0", "var0_mm", "ln0", "rstd0", "xh0", "x0",
    "x0b", "first", "xs1", "mean1_mm", "d1", "sq1", "sqs1", "var1_mm", "ln1", "rstd1", "xh1", "xn1", "sx1",
    "z", "w1_mm", "xxx", "w2_mm", "mix", "x5", "dec1_mm", "dec1", "dec2_mm", "e", "w", "v1_mm", "v1", "v_out",
    "vrep", "k1_mm", "k1", "r1_mm", "r1", "g_mm", "gth", "gg", "ruk", "ruk_mm", "bonus",
    "rest", "a", "s", "rs", "acc_mm", "sqg", "varg_mm", "lng", "rstdg", "xhg", "yg0", "yg", "wo1_mm", "x2",
    "xs2", "mean2_mm", "d2", "sq2", "sqs2", "var2_mm", "ln2", "rstd2", "xh2", "xn2", "sx2", "xr", "xk",
    "fr_mm", "rth", "fk_mm", "krelu", "kk", "fv_mm", "rk", "out", "out_st"]


def xattn_rwkv(nc, xT, cT, mask, first, rest, consts, w0, w1, vec, outT):
    ctx = ExitStack()
    with ctx:
        def sb(name, cols, dt=F32):
            return ctx.enter_context(nc.sbuf_tensor(name, [P, cols], dt))

        S = {n: ctx.enter_context(nc.semaphore("s_" + n)) for n in SEMS}

        cst = sb("cst", CONST_COLS)
        C = {n: cst[:, k * P:(k + 1) * P] for k, n in enumerate(CONST)}
        bdmask = cst[:, len(CONST) * P:CONST_COLS]
        w0_sb = sb("w0_sb", sum(W0_COLS.values()))
        w1_sb = sb("w1_sb", sum(W1_COLS.values()))
        W = {}
        for tile, cols in ((w0_sb, W0_COLS), (w1_sb, W1_COLS)):
            at = 0
            for n, k in cols.items():
                W[n] = tile[:, at:at + k]
                at += k
        vec_sb = sb("vec_sb", 2 * len(VEC))

        def V(name, c):
            k = 2 * VEC.index(name) + c
            return vec_sb[:, k:k + 1]

        def Wc(name, c, lo=0, n=P):
            return W[name].rearrange("p (c n) -> p c n", c=2)[:, c, lo:lo + n]

        bqs = sb("bqs", 2)
        eps = sb("eps", 2)
        ones = sb("ones", 1)
        maskid = sb("maskid", P, BF16)

        xq = sb("xq", CM)
        c_ = sb("c_", CM)
        cdup = sb("cdup", 2 * CM)
        mraw = sb("mraw", TOK)
        mres = sb("mres", TOK)
        mmid = sb("mmid", TOK, BF16)
        mhm = sb("mhm", TOK, BF16)
        mlo = sb("mlo", TOK, BF16)
        q2 = sb("q2", 2 * NB * P)
        kT = sb("kT", TOK)
        kbd = sb("kbd", NB * GROUP)
        vbd = sb("vbd", NB * KV * SV)
        x = sb("x", CM)
        prob = [sb(f"prob{k}", 2 * GROUP) for k in range(2)]
        probT = [sb(f"probT{k}", 2 * GROUP) for k in range(2)]
        mx = sb("mx", 4 * KV)
        rcp = sb("rcp", 2 * KV)
        o = sb("o", P)
        oT = sb("oT", CM)
        u = sb("u", CM)
        us = sb("us", TOK)
        d0 = u
        sq0 = sb("sq0", CM)
        sqs0 = sb("sqs0", TOK)
        lnv0 = sb("lnv0", TOK)
        rstd0 = sb("rstd0", TOK)
        x0 = sb("x0", CM)
        row1 = sb("row1", FIRST)
        xs1 = sb("xs1", TOK)
        d1 = sb("d1", CM)
        sq1 = sb("sq1", CM)
        sqs1 = sb("sqs1", TOK)
        lnv1 = sb("lnv1", TOK)
        rstd1 = sb("rstd1", TOK)
        xn1 = sb("xn1", 2 * NB * (L + 1))
        sx1 = sb("sx1", CM)
        z = sq1
        xxx = sb("xxx", CM)
        mix = [sb(f"mix{n}", CM) for n in range(5)]
        dec = sb("dec", TOK)
        e = z
        v1 = sb("v1", CM)
        gth = sb("gth", CM)
        ruk = e
        x0b = sb("x0b", CM)
        wsh = sb("wsh", 2 * CM)
        k1 = sb("k1", CM)
        r1 = sb("r1", CM)
        gg = sb("gg", CM)
        bonus = sb("bonus", CM)
        vrep = sb("vrep", HS * CM)
        restr = sb("restr", REST)
        a_all = sb("a_all", HS * CM)
        state = [sb(f"state{n}", 2 * CM) for n in range(2)]
        rs = state
        lng = sb("lng", CM)
        rstdg = sb("rstdg", CM)
        xhg = sb("xhg", CM)
        yg = xhg
        x2 = sb("x2", CM)
        xs2 = sb("xs2", TOK)
        d2 = sb("d2", CM)
        sq2 = sb("sq2", CM)
        sqs2 = sb("sqs2", TOK)
        lnv2 = sb("lnv2", TOK)
        rstd2 = sb("rstd2", TOK)
        xn2 = sb("xn2", 2 * NB * (L + 1))
        sx2 = sb("sx2", CM)
        xk = sq2
        xr = d2
        rth = sb("rth", CM)
        rk = res = rth
        krelu = sb("krelu", CM)
        kk = krelu
        scratch = nc.dram_tensor("v_scratch", [P, CM], F32).ap()

        bank = [ctx.enter_context(nc.psum_tensor(f"bank{k}", [P, 512], F32)) for k in range(8)]
        SC = bank[0:2]
        TR = bank[2]
        M0 = bank[3]
        RA, RB = bank[4], bank[5]
        RC = bank[6]
        ACC = bank[7]

        def two(ap):
            return ap.rearrange("p (c n) -> p c n", c=2)

        def both(ap):
            return ap.unsqueeze(1).broadcast_to([P, 2, TOK])

        def seqs(ap):
            return ap.rearrange("p (b t) -> p b t", t=L)

        def now(ap):
            return ap.rearrange("p (b t) -> p b t", b=2 * NB)[:, :, 1:L + 1]

        def before(ap):
            return ap.rearrange("p (b t) -> p b t", b=2 * NB)[:, :, 0:L]

        def half(ap, c):
            return two(ap)[:, c, :]

        def now_half(ap, c):
            return now(ap)[:, c * NB:(c + 1) * NB, :]

        def columns(tile, d):
            return tile[:, 2 * d * CM:2 * (d + 1) * CM].rearrange("p (d b t) -> p d b t", d=2, t=L)

        def for_both_columns(ap):
            return seqs(ap).unsqueeze(1).broadcast_to([P, 2, 2 * NB, L])

        def weights_ready(eng):
            eng.wait_ge(S["w_in"], 48)
            eng.wait_ge(S["ready"], 4)

        def all_steps(eng, slot):
            slot(0, None, None, None)
            slot(1, 0, None, None)
            slot(2, 1, 0, None)
            slot(3, 2, 1, 0)
            with eng.Fori(4, STEPS) as n:
                slot(n, n - 1, n - 2, n - 3)
            slot(None, STEPS - 1, STEPS - 2, STEPS - 3)
            slot(None, None, STEPS - 1, STEPS - 2)
            slot(None, None, None, STEPS - 1)

        block = ctx.enter_context(nc.Block())

        @block.sync
        def _(sp):
            def rows(array, n):
                return array[bass.ds(n, 1), :, :].rearrange("a p n -> (a p) n")

            def load_pre(i):
                sp.wait_ge(S["k_mm"], i)
                sp.wait_ge(S["cdup"], i)
                sp.dma_start(c_[:, :], rows(cT, i)).then_inc(S["c_in"], 16)
                sp.wait_ge(S["mask2"], i)
                for h in range(2):
                    sp.dma_start(mraw[64 * h:64 * h + 64, :], rows(mask, i)).then_inc(S["m_in"], 16)
                sp.wait_ge(S["q_mm"], i)
                sp.dma_start(xq[:, :], rows(xT, i)).then_inc(S["xq_in"], 16)

            def slot(pre, att, low, top):
                if pre is not None:
                    load_pre(pre)
                if att is None and low is None and top is None:
                    sp.dma_start(w1_sb[:, :], w1).then_inc(S["w1_in"], 16)
                if att is not None:
                    src = rows(xT, att)
                    sp.wait_ge(S["u"], 2 * att)
                    sp.dma_start(x[:, :], src).then_inc(S["x_in"], 16)
                if low is not None:
                    src = rows(first, low)
                    sp.wait_ge(S["first"], low)
                    sp.dma_start(row1[:, :], src).then_inc(S["first_in"], 16)
                if top is not None:
                    src = rows(rest, top)
                    sp.wait_ge(S["rest"], 2 * top)
                    sp.dma_start(restr[:, :], src).then_inc(S["rest_in"], 16)
                if low is not None:
                    sp.wait_ge(S["v1"], low + 1)
                    sp.dma_start(scratch, v1[:, :]).then_inc(S["v_out"], 16)
                    sp.wait_ge(S["v_out"], 16 * (low + 1))
                    sp.dma_start(vrep[:, :], scratch.rearrange("(h d) n -> h (d n)", d=HS).unsqueeze(1)
                                 .broadcast_to([P // HS, HS, HS * CM])).then_inc(S["vrep"], 16)
                if top is not None:
                    dst = rows(outT, top)
                    sp.wait_ge(S["out"], top + 1)
                    sp.dma_start(dst, res[:, :]).then_inc(S["out_st"], 16)

            sp.dma_start(w0_sb[:, :], w0).then_inc(S["w_in"], 16)
            sp.dma_start(vec_sb[:, :], vec).then_inc(S["w_in"], 16)
            sp.dma_start(cst[:, :], consts).then_inc(S["w_in"], 16)
            all_steps(sp, slot)
            sp.wait_ge(S["out_st"], 16 * STEPS)

        @block.tensor
        def _(pe):
            def mm(out, lhsT, rhs, start=True, stop=True):
                return nc.tensor.matmul(out, lhsT, rhs, start=start, stop=stop, skip_group_check=True)

            def dense(out, name, rhs):
                for m in range(2):
                    for c in range(2):
                        last = mm(two(out)[:, m, :], Wc(name, c, m * P), half(rhs, c), c == 0, c == 1)
                return last

            def k_proj(i):
                pe.wait_ge(S["c_in"], 16 * (i + 1))
                pe.wait_ge(S["sub"], 8 * i)
                for c in range(2):
                    last = mm(SC[0][:, 0:TOK], Wc("wk", c), half(c_[:, :], c), c == 0, c == 1)
                last.then_inc(S["k_mm"], 1)

            def q_proj(i):
                pe.wait_ge(S["xq_in"], 16 * (i + 1))
                dense(SC[1][:, :], "wq", xq[:, :]).then_inc(S["q_mm"], 1)

            def v_proj(i):
                pe.wait_ge(S["cdup"], i + 1)
                pe.wait_ge(S["pt_ev"], 8 * i)
                for b in range(NB):
                    for c in range(2):
                        n = (c * NB + b) * P
                        last = mm(TR[:, b * 64:(b + 1) * 64], cdup[:, n:n + P],
                                  W["wv"].rearrange("p (c n) -> p c n", c=2)[:, c, :], c == 0, c == 1)
                last.then_inc(S["v_mm"], 1)

            def qk(i, b):
                pe.wait_ge(S["kbd"], NB * i + b + 1)
                if b == 0:
                    pe.wait_ge(S["q_ev"], 4 * (i + 1))
                    pe.wait_ge(S["mask5"], i + 1)
                    pe.wait_ge(S["k_ev"], i + 1)
                for gp in range(2):
                    if b > 0:
                        pe.wait_ge(S["sub"], 8 * i + 2 * (b - 1) + gp + 1)
                    n = (gp * NB + b) * P
                    mm(SC[gp][:, :], q2[:, n:n + P], kbd[:, b * GROUP:(b + 1) * GROUP], True, False)
                    for part in (mhm, mlo):
                        m = part[:, b * L:(b + 1) * L].unsqueeze(1).broadcast_to([P, KV, L])
                        last = mm(SC[gp][:, :].rearrange("p (k s) -> p k s", k=KV), maskid[:, :], m, False, part is mlo)
                    last.then_inc(S["qk_mm"], 1)

            def tr(i, b, gp):
                n = 8 * i + 2 * b + gp
                if gp == 0:
                    pe.wait_ge(S["exp"], NB * i + b + 1)
                if b == 0 and gp == 0:
                    pe.wait_ge(S["v_ev"], 2 * (i + 1))
                else:
                    pe.wait_ge(S["pt_ev"], n)
                for p in range(4):
                    at = gp * GROUP + p * P
                    last = nc.tensor.transpose(TR[:, p * P:(p + 1) * P], prob[b % 2][:, at:at + P], C["ident"])
                last.then_inc(S["tr_mm"], 1)

            def pv(i, b):
                pe.wait_ge(S["pt_ev"], 8 * i + 2 * b + 2)
                if b == 0:
                    pe.wait_ge(S["ln0"], i)
                else:
                    pe.wait_ge(S["ot_ev"], NB * i + b)
                for gp in range(2):
                    for p in range(4):
                        n = (gp * 4 + p) * 2 * SV
                        at = gp * GROUP + p * P
                        last = mm(M0[:, n:n + 2 * SV], probT[b % 2][:, at:at + P],
                                  vbd[:, (b * 4 + p) * 2 * SV:(b * 4 + p + 1) * 2 * SV])
                last.then_inc(S["pv_mm"], 1)

            def otr(i, b):
                pe.wait_ge(S["o_ev"], NB * i + b + 1)
                nc.tensor.transpose(M0[:, 256:256 + P], o[:, :], C["ident"]).then_inc(S["ot_mm"], 1)

            def wo(i):
                pe.wait_ge(S["ot_ev"], NB * (i + 1))
                dense(M0[:, :], "wo", oT[:, :]).then_inc(S["wo_mm"], 1)

            def mean0(i):
                pe.wait_ge(S["us"], i + 1)
                mm(M0[:, 0:TOK], C["mean256"], us[:, :]).then_inc(S["mean0_mm"], 1)

            def var0(i):
                pe.wait_ge(S["sqs0"], i + 1)
                mm(M0[:, 0:TOK], C["mean256"], sqs0[:, :]).then_inc(S["var0_mm"], 1)

            def mean1(j):
                pe.wait_ge(S["xs1"], j + 1)
                pe.wait_ge(S["bonus"], j)
                mm(RA[:, 0:TOK], C["mean256"], xs1[:, :]).then_inc(S["mean1_mm"], 1)

            def var1(j):
                pe.wait_ge(S["sqs1"], j + 1)
                pe.wait_ge(S["gg"], j)
                mm(RB[:, 0:TOK], C["mean256"], sqs1[:, :]).then_inc(S["var1_mm"], 1)

            def w1mm(j):
                pe.wait_ge(S["w1_in"], 16)
                pe.wait_ge(S["z"], 2 * (j + 1))
                for lo, n in ((0, P), (P, 32)):
                    for c in range(2):
                        last = mm(RA[0:n, 2 * lo:2 * lo + TOK], Wc("w1", c, lo, n), half(z[:, :], c), c == 0, c == 1)
                last.then_inc(S["w1_mm"], 1)

            def w2mm(j, k):
                n = MIXES[k]
                bk = (RB, RA, RA, RB, RB)[k]
                if k == 0:
                    pe.wait_ge(S["xxx"], 2 * (j + 1))
                    pe.wait_ge(S["ln1"], j + 1)
                if k == 2:
                    pe.wait_ge(S["mix"], 10 * j + 4)
                if k == 3:
                    pe.wait_ge(S["v1"], j + 1)
                if k == 4:
                    pe.wait_ge(S["mix"], 10 * j + 8)
                lhs = W["w2"][32 * n:32 * n + 32, :] if n < 4 else W["w2b"][0:32, :]
                rhs = xxx[32 * n:32 * n + 32, 0:TOK] if n < 4 else xxx[0:32, TOK:CM]
                for m in range(2):
                    last = mm(two(bk[:, :])[:, m, :], lhs[:, m * P:(m + 1) * P], rhs)
                last.then_inc(S["w2_mm"], 1)

            def dec1(j):
                pe.wait_ge(S["x5"], 5 * j + 1)
                for c in range(2):
                    last = mm(RB[0:64, 0:TOK], Wc("dw1", c, 0, 64), half(mix[1][:, :], c), c == 0, c == 1)
                last.then_inc(S["dec1_mm"], 1)

            def v1mm(j):
                pe.wait_ge(S["x5"], 5 * j + 2)
                pe.wait_ge(S["dec1"], j + 1)
                dense(RB[:, :], "wvv", mix[2][:, :]).then_inc(S["v1_mm"], 1)

            def dec2(j):
                pe.wait_ge(S["dec1"], j + 1)
                pe.wait_ge(S["mix"], 10 * j + 6)
                for m in range(2):
                    last = mm(two(RA[:, :])[:, m, :], W["dw2"][0:64, m * P:(m + 1) * P], dec[0:64, :])
                last.then_inc(S["dec2_mm"], 1)

            def k1mm(j):
                pe.wait_ge(S["x5"], 5 * j + 3)
                pe.wait_ge(S["e"], 2 * (j + 1))
                dense(RA[:, :], "wkk", mix[0][:, :]).then_inc(S["k1_mm"], 1)

            def r1mm(j):
                pe.wait_ge(S["x5"], 5 * j + 4)
                pe.wait_ge(S["k1"], j + 1)
                dense(RA[:, :], "wr", mix[3][:, :]).then_inc(S["r1_mm"], 1)

            def gmm(j):
                pe.wait_ge(S["x5"], 5 * j + 5)
                dense(RB[:, :], "wg", mix[4][:, :]).then_inc(S["g_mm"], 1)

            def rukmm(j):
                pe.wait_ge(S["ruk"], 2 * (j + 1))
                mm(RA[:, :], C["sum8"], ruk[:, :]).then_inc(S["ruk_mm"], 1)

            def acc_bonus(h):
                pe.wait_ge(S["bonus"], h + 1)
                pe.wait_ge(S["kk"], h)
                mm(ACC[:, :], C["center8"], bonus[:, :], True, False)

            def acc(h, d):
                pe.wait_ge(S["rs"], PAIRS * h + d + 1)
                for k in range(2):
                    last = mm(ACC[:, :], C[f"red{2 * d + k}"], rs[d % 2][:, k * CM:(k + 1) * CM], False,
                              d == PAIRS - 1 and k == 1)
                last.then_inc(S["acc_mm"], 1)

            def varg(h):
                pe.wait_ge(S["sqg"], h + 1)
                pe.wait_ge(S["rk"], h)
                mm(RC[:, :], C["mean8"], sq2[:, :]).then_inc(S["varg_mm"], 1)

            def wo1(h):
                pe.wait_ge(S["yg"], h + 1)
                dense(ACC[:, :], "woo", yg[:, :]).then_inc(S["wo1_mm"], 1)

            def mean2(h):
                pe.wait_ge(S["xs2"], h + 1)
                mm(RC[:, 0:TOK], C["mean256"], xs2[:, :]).then_inc(S["mean2_mm"], 1)

            def var2(h):
                pe.wait_ge(S["sqs2"], h + 1)
                mm(ACC[:, 0:TOK], C["mean256"], sqs2[:, :]).then_inc(S["var2_mm"], 1)

            def frmm(h):
                pe.wait_ge(S["xr"], 2 * (h + 1))
                dense(RC[:, :], "fr", xr[:, :]).then_inc(S["fr_mm"], 1)

            def fkmm(h):
                pe.wait_ge(S["xk"], 2 * (h + 1))
                dense(ACC[:, :], "fk", xk[:, :]).then_inc(S["fk_mm"], 1)

            def fvmm(h):
                pe.wait_ge(S["kk"], h + 1)
                pe.wait_ge(S["rth"], h + 1)
                dense(RC[:, :], "fv", kk[:, :]).then_inc(S["fv_mm"], 1)

            def slot(pre, att, low, top):
                Q, A, Z, T = (n is not None for n in (pre, att, low, top))
                if A: qk(att, 0)
                if Z: mean1(low)
                if A: qk(att, 1)
                if A: tr(att, 0, 0)
                if A: qk(att, 2)
                if A: tr(att, 0, 1)
                if T: acc_bonus(top)
                if Z: var1(low)
                if A: pv(att, 0)
                if A: tr(att, 1, 0)
                if A: qk(att, 3)
                if A: tr(att, 1, 1)
                if A: otr(att, 0)
                if T: acc(top, 0)
                if Z: w1mm(low)
                if A: tr(att, 2, 0)
                if A: pv(att, 1)
                if A: tr(att, 2, 1)
                if Q: k_proj(pre)
                if T: acc(top, 1)
                if Z: w2mm(low, 0)
                if Z: w2mm(low, 1)
                if Q: q_proj(pre)
                if T: acc(top, 2)
                if T: acc(top, 3)
                if A: otr(att, 1)
                if A: tr(att, 3, 0)
                if Z: dec1(low)
                if T: varg(top)
                if A: pv(att, 2)
                if A: tr(att, 3, 1)
                if Z: w2mm(low, 2)
                if Z: v1mm(low)
                if A: otr(att, 2)
                if Z: dec2(low)
                if T: wo1(top)
                if Z: w2mm(low, 3)
                if A: pv(att, 3)
                if T: mean2(top)
                if Z: k1mm(low)
                if A: otr(att, 3)
                if Z: w2mm(low, 4)
                if T: var2(top)
                if A: wo(att)
                if Z: r1mm(low)
                if Z: gmm(low)
                if A: mean0(att)
                if T: frmm(top)
                if T: fkmm(top)
                if Q: v_proj(pre)
                if Z: rukmm(low)
                if A: var0(att)
                if T: fvmm(top)

            weights_ready(pe)
            all_steps(pe, slot)

        @block.vector
        def _(dve):
            v = nc.vector

            def k_ev(i):
                dve.wait_ge(S["k_mm"], i + 1)
                dve.wait_ge(S["kbd"], NB * i)
                v.tensor_scalar(kT[:, :], SC[0][:, 0:TOK], V("bk", 0), None, ALU.add).then_inc(S["k_ev"], 1)

            def v_ev(i):
                dve.wait_ge(S["v_mm"], i + 1)
                for h in range(2):
                    rows = slice(64 * h, 64 * h + 64)
                    src = TR[rows, 0:NB * 64].rearrange("p (b k d) -> p b k d", b=NB, k=KV)[:, :, h::2, :]
                    dst = vbd[rows, :].rearrange("p (b k d) -> p b k d", b=NB, k=KV)[:, :, h::2, 0:HD]
                    bias = W["bv"][rows, :].rearrange("p (k d) -> p k d", k=KV)[:, h::2, :]\
                        .unsqueeze(1).broadcast_to([64, NB, KV // 2, HD])
                    v.tensor_tensor(dst, src, bias, ALU.add).then_inc(S["v_ev"], 1)

            def softmax(i, b):
                for gp in range(2):
                    n = 8 * i + 2 * b + gp
                    sc = SC[gp][:, :].rearrange("p (k s) -> p k s", k=KV)
                    m = mx[:, (2 * (b % 2) + gp) * KV:(2 * (b % 2) + gp + 1) * KV]
                    dve.wait_ge(S["qk_mm"], n + 1)
                    v.tensor_reduce(m, sc, AXX, ALU.max).then_inc(S["mx"], 1)
                    if b >= 2:
                        dve.wait_ge(S["tr_mm"], n - 3)
                    dve.wait_ge(S["mx"], n + 1)
                    v.tensor_tensor(prob[b % 2][:, gp * GROUP:(gp + 1) * GROUP]
                                    .rearrange("p (k s) -> p k s", k=KV), sc,
                                    m.unsqueeze(2).broadcast_to([P, KV, L]), ALU.subtract).then_inc(S["sub"], 1)

            def o_ev(i, b):
                n = NB * i + b + 1
                pvv = M0[:, 0:2 * KV * SV].rearrange("p (k d) -> p k d", d=SV)
                dve.wait_ge(S["pv_mm"], n)
                v.reciprocal(rcp[:, :], pvv[:, :, HD:SV].rearrange("p k d -> p (k d)")).then_inc(S["rcp"], 1)
                dve.wait_ge(S["ot_mm"], n - 1)
                dve.wait_ge(S["rcp"], n)
                v.tensor_tensor(o[:, :].rearrange("p (k d) -> p k d", d=HD), pvv[:, :, 0:HD],
                                rcp[:, :].unsqueeze(2).broadcast_to([P, 2 * KV, HD]), ALU.mult).then_inc(S["o_ev"], 1)

            def residual0(i):
                dve.wait_ge(S["x_in"], 16 * (i + 1))
                dve.wait_ge(S["wo_mm"], i + 1)
                for c in range(2):
                    v.scalar_tensor_tensor(half(u[:, :], c), half(M0[:, :], c), V("bo", c), half(x[:, :], c),
                                           ALU.add, ALU.add).then_inc(S["u"], 1)

            def center(n, mean_mm, bk, src, dst, done):
                dve.wait_ge(S[mean_mm], n + 1)
                v.tensor_tensor(two(dst[:, :]), two(src[:, :]), both(bk[:, 0:TOK]), ALU.subtract).then_inc(S[done], 1)

            def normal(n, rstd_done, src, rstd, done):
                dve.wait_ge(S[rstd_done], n + 1)
                v.tensor_tensor(two(src[:, :]), two(src[:, :]), both(rstd[:, 0:TOK]), ALU.mult).then_inc(S[done], 1)

            def mixin(xn, sx, name, dst, done):
                for c in range(2):
                    v.scalar_tensor_tensor(seqs(half(dst[:, :], c)), seqs(half(sx[:, :], c)), V(name, c),
                                           now_half(xn, c), ALU.mult, ALU.add).then_inc(S[done], 1)

            def zmix(j):
                dve.wait_ge(S["sx1"], j + 1)
                mixin(xn1[:, :], sx1, "maax", z, "z")

            def mixes(j, k):
                n = MIXES[k]
                bk = (RB, RA, RA, RB, RB)[k]
                dve.wait_ge(S["w2_mm"], 5 * j + k + 1)
                for c in range(2):
                    v.scalar_tensor_tensor(half(mix[n][:, :], c), half(bk[:, :], c), V(f"maa{n}", c),
                                           half(sx1[:, :], c), ALU.add, ALU.mult).then_inc(S["mix"], 1)

            def ggate(j):
                dve.wait_ge(S["gth"], j + 1)
                v.scalar_tensor_tensor(gg[:, :], gth[:, :], 1.0, RB[:, :], ALU.add, ALU.mult).then_inc(S["gg"], 1)

            def rukf(j):
                dve.wait_ge(S["r1"], j + 1)
                for c in range(2):
                    v.scalar_tensor_tensor(half(ruk[:, :], c), half(k1[:, :], c), V("u", c), half(r1[:, :], c),
                                           ALU.mult, ALU.mult).then_inc(S["ruk"], 1)

            def bonusf(j):
                dve.wait_ge(S["ruk_mm"], j + 1)
                dve.wait_ge(S["acc_mm"], PAIRS * j)
                v.tensor_tensor(bonus[:, :], RA[:, :], v1[:, :], ALU.mult).then_inc(S["bonus"], 1)

            def outer(h, d):
                if d == 0:
                    dve.wait_ge(S["k1"], h + 1)
                    dve.wait_ge(S["vrep"], 16 * (h + 1))
                v.tensor_tensor(columns(a_all, d)[:, :, :, 1:L], for_both_columns(k1[:, :])[:, :, :, 0:L - 1],
                                columns(vrep, d)[:, :, :, 0:L - 1], ALU.mult).then_inc(S["a"], 1)

            def scan(h, d):
                n = PAIRS * h + d + 1
                if d == 0:
                    dve.wait_ge(S["rest"], 2 * (h + 1))
                    dve.wait_ge(S["w"], 2 * (h + 1))
                if d >= 2:
                    dve.wait_ge(S["acc_mm"], n - 2)
                dve.wait_ge(S["a"], n)
                v.tensor_tensor_scan(state[d % 2][:, :], wsh[:, :], a_all[:, 2 * d * CM:2 * (d + 1) * CM], 0.0,
                                     ALU.mult, ALU.add).then_inc(S["s"], 1)

            def receive(h, d):
                n = PAIRS * h + d + 1
                dve.wait_ge(S["s"], n)
                v.tensor_tensor(columns(rs[d % 2], 0), for_both_columns(r1[:, :]), columns(state[d % 2], 0),
                                ALU.mult).then_inc(S["rs"], 1)

            def xhgf(h):
                dve.wait_ge(S["rstdg"], h + 1)
                v.tensor_tensor(xhg[:, :], ACC[:, :], rstdg[:, :], ALU.mult).then_inc(S["xhg"], 1)

            def gate(h):
                dve.wait_ge(S["yg0"], 2 * (h + 1))
                v.tensor_tensor(yg[:, :], xhg[:, :], gg[:, :], ALU.mult).then_inc(S["yg"], 1)

            def res2(h):
                dve.wait_ge(S["x0b"], h + 1)
                dve.wait_ge(S["wo1_mm"], h + 1)
                v.scalar_tensor_tensor(x2[:, :], ACC[:, :], 0.5, x0b[:, :], ALU.mult, ALU.add).then_inc(S["x2"], 1)

            def ffn_mix(h):
                dve.wait_ge(S["sx2"], h + 1)
                mixin(xn2[:, :], sx2, "fmr", xr, "xr")
                mixin(xn2[:, :], sx2, "fmk", xk, "xk")

            def kkf(h):
                dve.wait_ge(S["krelu"], h + 1)
                v.tensor_tensor(kk[:, :], krelu[:, :], ACC[:, :], ALU.mult).then_inc(S["kk"], 1)

            def rkf(h):
                dve.wait_ge(S["fv_mm"], h + 1)
                v.scalar_tensor_tensor(rk[:, :], rth[:, :], 1.0, RC[:, :], ALU.add, ALU.mult).then_inc(S["rk"], 1)

            def outf(h):
                dve.wait_ge(S["rk"], h + 1)
                v.scalar_tensor_tensor(res[:, :], rk[:, :], 0.5, x2[:, :], ALU.mult, ALU.add).then_inc(S["out"], 1)

            def slot(pre, att, low, top):
                Q, A, Z, T = (n is not None for n in (pre, att, low, top))
                if A: softmax(att, 0)
                if Z: center(low, "mean1_mm", RA, x0, d1, "d1")
                if A: softmax(att, 1)
                if T: outer(top, 0)
                if T: scan(top, 0)
                if A: softmax(att, 2)
                if Z: normal(low, "rstd1", d1, rstd1, "xh1")
                if T: outer(top, 1)
                if A: o_ev(att, 0)
                if T: receive(top, 0)
                if Z: zmix(low)
                if A: softmax(att, 3)
                if T: scan(top, 1)
                if T: outer(top, 2)
                if T: receive(top, 1)
                if T: scan(top, 2)
                if T: receive(top, 2)
                if T: outer(top, 3)
                if T: scan(top, 3)
                if T: receive(top, 3)
                if Q: k_ev(pre)
                if Z: mixes(low, 0)
                if A: o_ev(att, 1)
                if Z: mixes(low, 1)
                if A: o_ev(att, 2)
                if T: xhgf(top)
                if Z: mixes(low, 2)
                if T: gate(top)
                if T: res2(top)
                if Z: mixes(low, 3)
                if A: o_ev(att, 3)
                if T: center(top, "mean2_mm", RC, x2, d2, "d2")
                if Z: mixes(low, 4)
                if T: normal(top, "rstd2", d2, rstd2, "xh2")
                if A: residual0(att)
                if T: ffn_mix(top)
                if Z: rukf(low)
                if A: center(att, "mean0_mm", M0, u, d0, "d0")
                if T: kkf(top)
                if Q: v_ev(pre)
                if Z: ggate(low)
                if Z: bonusf(low)
                if A: normal(att, "rstd0", d0, rstd0, "xh0")
                if T: rkf(top)
                if T: outf(top)

            v.memset(q2[:, :], 0.0).then_inc(S["ready"], 1)
            v.memset(vbd[:, :], 0.0).then_inc(S["ready"], 1)
            v.memset(eps[:, 0:1], EPS0)
            v.memset(eps[:, 1:2], EPS1)
            v.memset(ones[:, :], 1.0)
            dve.wait_ge(S["w_in"], 48)
            v.tensor_scalar(bqs[:, :], vec_sb[:, 0:2], SCALE, None, ALU.mult)
            dve.wait_ge(S["ready"], 2)
            for h in range(2):
                rows = slice(64 * h, 64 * h + 64)
                last = v.memset(vbd[rows, :].rearrange("p (b k d) -> p b k d", b=NB, k=KV)[:, :, h::2, HD:SV], 1.0)
            last.then_inc(S["ready"], 1)
            v.memset(seqs(wsh[:, :])[:, :, 0:1], 0.0)
            v.memset(mlo[64:P, :], 0.0)
            v.tensor_copy(maskid[:, :], C["maskid"]).then_inc(S["ready"], 1)
            weights_ready(dve)
            all_steps(dve, slot)

        @block.scalar
        def _(act):
            s = nc.scalar

            def q_ev(i):
                act.wait_ge(S["q_mm"], i + 1)
                for gp in range(2):
                    for h in range(2):
                        rows = slice(64 * h, 64 * h + 64)
                        dst = q2[rows, :].rearrange("p (g b h t) -> p g b h t", g=2, b=NB, h=2)[:, gp, :, h, :]
                        s.activation(dst, seqs(SC[1][rows, gp * TOK:(gp + 1) * TOK]), ACT.Identity,
                                     bias=bqs[rows, gp:gp + 1], scale=SCALE).then_inc(S["q_ev"], 1)

            def expo(i, b):
                act.wait_ge(S["sub"], 8 * i + 2 * b + 2)
                s.activation(prob[b % 2][:, :], prob[b % 2][:, :], ACT.Exp).then_inc(S["exp"], 1)

            def pt_ev(i, b, gp):
                act.wait_ge(S["tr_mm"], 8 * i + 2 * b + gp + 1)
                s.copy(probT[b % 2][:, gp * GROUP:(gp + 1) * GROUP], TR[:, :]).then_inc(S["pt_ev"], 1)

            def ot_ev(i, b):
                act.wait_ge(S["ot_mm"], NB * i + b + 1)
                s.copy(oT[:, :].rearrange("p (h b t) -> p h b t", h=2, b=NB)[:, :, b, :],
                       M0[:, 256:256 + P].rearrange("p (h t) -> p h t", h=2)).then_inc(S["ot_ev"], 1)

            def square(n, after, src, dst, done, times=1):
                act.wait_ge(S[after], times * (n + 1))
                s.activation(dst[:, :], src[:, :], ACT.Square).then_inc(S[done], 1)

            def rsqrt(n, after, bk, k, lnv, rstd, ln_done, done):
                act.wait_ge(S[after], n + 1)
                s.activation(lnv[:, :], bk[:, 0:lnv.shape[1]], ACT.Ln, bias=eps[:, k:k + 1]).then_inc(S[ln_done], 1)
                act.wait_ge(S[ln_done], n + 1)
                s.activation(rstd[:, :], lnv[:, :], ACT.Exp, scale=-0.5).then_inc(S[done], 1)

            def affine(src, dst_half, w, b, done):
                for c in range(2):
                    s.activation(dst_half(c), seqs(half(src[:, :], c)), ACT.Identity, bias=V(b, c), scale=V(w, c))\
                        .then_inc(S[done], 1)

            def xn1f(j):
                act.wait_ge(S["xh1"], j + 1)
                act.wait_ge(S["x5"], 5 * j)
                affine(d1, lambda c: now_half(xn1[:, :], c), "ln1w", "ln1b", "xn1")

            def xxxf(j):
                act.wait_ge(S["w1_mm"], j + 1)
                s.activation(xxx[:, 0:TOK], RA[:, 0:TOK], ACT.Tanh).then_inc(S["xxx"], 1)
                s.activation(xxx[0:32, TOK:CM], RA[0:32, TOK:CM], ACT.Tanh).then_inc(S["xxx"], 1)

            def decf(j):
                act.wait_ge(S["dec1_mm"], j + 1)
                s.activation(dec[0:64, :], RB[0:64, 0:TOK], ACT.Tanh).then_inc(S["dec1"], 1)

            def v1f(j):
                act.wait_ge(S["v1_mm"], j + 1)
                act.wait_ge(S["a"], PAIRS * j)
                act.wait_ge(S["bonus"], j)
                s.copy(v1[:, :], RB[:, :]).then_inc(S["v1"], 1)

            def wf(j):
                act.wait_ge(S["dec2_mm"], j + 1)
                for c in range(2):
                    s.activation(half(e[:, :], c), half(RA[:, :], c), ACT.Exp, bias=V("td", c)).then_inc(S["e"], 1)
                act.wait_ge(S["s"], PAIRS * j)
                act.wait_ge(S["e"], 2 * (j + 1))
                for k in range(2):
                    s.activation(seqs(wsh[:, k * CM:(k + 1) * CM])[:, :, 1:L], seqs(e[:, :])[:, :, 0:L - 1], ACT.Exp,
                                 scale=-1.0).then_inc(S["w"], 1)

            def k1f(j):
                act.wait_ge(S["a"], PAIRS * j)
                act.wait_ge(S["k1_mm"], j + 1)
                s.copy(k1[:, :], RA[:, :]).then_inc(S["k1"], 1)

            def r1f(j):
                act.wait_ge(S["rs"], PAIRS * j)
                act.wait_ge(S["r1_mm"], j + 1)
                s.copy(r1[:, :], RA[:, :]).then_inc(S["r1"], 1)

            def gthf(j):
                act.wait_ge(S["g_mm"], j + 1)
                s.activation(gth[:, :], RB[:, :], ACT.Tanh, scale=0.5).then_inc(S["gth"], 1)

            def sqgf(h):
                act.wait_ge(S["acc_mm"], PAIRS * (h + 1))
                s.activation(sq2[:, :], ACC[:, :], ACT.Square).then_inc(S["sqg"], 1)

            def yg0f(h):
                act.wait_ge(S["xhg"], h + 1)
                for c in range(2):
                    s.activation(half(xhg[:, :], c), half(xhg[:, :], c), ACT.Identity, bias=V("gnb", c),
                                 scale=V("gnw", c)).then_inc(S["yg0"], 1)

            def xn2f(h):
                act.wait_ge(S["xh2"], h + 1)
                affine(d2, lambda c: now_half(xn2[:, :], c), "ln2w", "ln2b", "xn2")

            def rthf(h):
                act.wait_ge(S["fr_mm"], h + 1)
                act.wait_ge(S["out_st"], 16 * h)
                s.activation(rth[:, :], RC[:, :], ACT.Tanh, scale=0.5).then_inc(S["rth"], 1)

            def kreluf(h):
                act.wait_ge(S["fk_mm"], h + 1)
                act.wait_ge(S["fv_mm"], h)
                s.activation(krelu[:, :], ACC[:, :], ACT.Relu).then_inc(S["krelu"], 1)

            def x0f(i):
                act.wait_ge(S["xh0"], i + 1)
                act.wait_ge(S["x0b"], i)
                act.wait_ge(S["d1"], i)
                affine(d0, lambda c: seqs(half(x0[:, :], c)), "gamma", "beta", "x0")

            def log_tables():
                s.preload_act_table_set("natural_log_exp_and_others")

            def slot(pre, att, low, top):
                Q, A, Z, T = (n is not None for n in (pre, att, low, top))
                if A: expo(att, 0)
                if Z: square(low, "d1", d1, sq1, "sq1")
                if A: pt_ev(att, 0, 0)
                if A: expo(att, 1)
                if A: pt_ev(att, 0, 1)
                if Z: rsqrt(low, "var1_mm", RB, 1, lnv1, rstd1, "ln1", "rstd1")
                if Z: xn1f(low)
                if A: pt_ev(att, 1, 0)
                if A: expo(att, 2)
                if A: pt_ev(att, 1, 1)
                if A: ot_ev(att, 0)
                if Z: xxxf(low)
                if A: pt_ev(att, 2, 0)
                if A: pt_ev(att, 2, 1)
                if A: expo(att, 3)
                if A: ot_ev(att, 1)
                if T: sqgf(top)
                if Z: decf(low)
                if A: pt_ev(att, 3, 0)
                log_tables()
                if T: rsqrt(top, "varg_mm", RC, 1, lng, rstdg, "lng", "rstdg")
                if T: yg0f(top)
                if A: pt_ev(att, 3, 1)
                if Z: v1f(low)
                if A: ot_ev(att, 2)
                if Z: wf(low)
                if T: square(top, "d2", d2, sq2, "sq2")
                if A: ot_ev(att, 3)
                if T: rsqrt(top, "var2_mm", ACC, 1, lnv2, rstd2, "ln2", "rstd2")
                if Z: k1f(low)
                if T: xn2f(top)
                if Q: q_ev(pre)
                if Z: r1f(low)
                if Z: gthf(low)
                if A: square(att, "d0", d0, sq0, "sq0")
                if T: rthf(top)
                if T: kreluf(top)
                log_tables()
                if A: rsqrt(att, "var0_mm", M0, 0, lnv0, rstd0, "ln0", "rstd0")
                if A: x0f(att)

            weights_ready(act)
            all_steps(act, slot)

        @block.gpsimd
        def _(pool):
            g = nc.gpsimd

            def copy(dst, src, rows=slice(0, P)):
                one = ones[rows, :]
                for _ in range(len(src.shape) - 2):
                    one = one.unsqueeze(1)
                return g.tensor_tensor(dst, src, one.broadcast_to(src.shape), ALU.mult)

            def split_mask(i):
                pool.wait_ge(S["m_in"], 32 * (i + 1))
                pool.wait_ge(S["qk_mm"], 8 * i)
                copy(mhm[:, :], mraw[:, :]).then_inc(S["mask1"], 1)
                pool.wait_ge(S["mask1"], i + 1)
                g.tensor_tensor(mres[:, :], mraw[:, :], mhm[:, :], ALU.subtract).then_inc(S["mask2"], 1)
                pool.wait_ge(S["mask2"], i + 1)
                copy(mmid[:, :], mres[:, :]).then_inc(S["mask3"], 1)
                pool.wait_ge(S["mask3"], i + 1)
                copy(mhm[64:P, :], mmid[64:P, :], slice(64, P)).then_inc(S["mask4"], 1)
                pool.wait_ge(S["mask4"], i + 1)
                g.tensor_tensor(mlo[0:64, :], mres[0:64, :], mmid[0:64, :], ALU.subtract).then_inc(S["mask5"], 1)
                pool.wait_ge(S["mask5"], i + 1)

            def duplicate(i):
                pool.wait_ge(S["c_in"], 16 * (i + 1))
                pool.wait_ge(S["v_mm"], i)
                copy(cdup[:, :].rearrange("p (b h t) -> p b h t", b=2 * NB, h=2),
                     seqs(c_[:, :]).unsqueeze(2).broadcast_to([P, 2 * NB, 2, L])).then_inc(S["cdup"], 1)

            def kbdf(i, b):
                pool.wait_ge(S["k_ev"], i + 1)
                k3 = [P, KV, L]
                g.tensor_tensor(kbd[:, b * GROUP:(b + 1) * GROUP].rearrange("p (k s) -> p k s", k=KV),
                                kT[:, b * L:(b + 1) * L].unsqueeze(1).broadcast_to(k3),
                                bdmask.unsqueeze(2).broadcast_to(k3), ALU.mult).then_inc(S["kbd"], 1)

            def fold(n, after, times, src, dst, done):
                pool.wait_ge(S[after], times * (n + 1))
                g.tensor_tensor(dst[:, :], half(src[:, :], 0), half(src[:, :], 1), ALU.add).then_inc(S[done], 1)

            def shift(j, after, xn, sx, done):
                pool.wait_ge(S[after], 2 * (j + 1))
                g.tensor_tensor(seqs(sx[:, :]), before(xn[:, :]), now(xn[:, :]), ALU.subtract).then_inc(S[done], 1)

            def row1f(j):
                pool.wait_ge(S["first_in"], 16 * (j + 1))
                copy(xn1[:, :].rearrange("p (b t) -> p b t", b=2 * NB)[:, :, 0:1], row1[:, :].unsqueeze(2))\
                    .then_inc(S["first"], 1)

            def restf(h):
                pool.wait_ge(S["rest_in"], 16 * (h + 1))
                pool.wait_ge(S["s"], PAIRS * h)
                copy(a_all[:, :].rearrange("p (d t) -> p d t", t=L)[:, :, 0:1], restr[:, FIRST:REST].unsqueeze(2))\
                    .then_inc(S["rest"], 1)
                pool.wait_ge(S["xk"], 2 * h)
                copy(xn2[:, :].rearrange("p (b t) -> p b t", b=2 * NB)[:, :, 0:1], restr[:, 0:FIRST].unsqueeze(2))\
                    .then_inc(S["rest"], 1)

            def x0bf(j):
                pool.wait_ge(S["x0"], 2 * (j + 1))
                pool.wait_ge(S["x2"], j)
                copy(x0b[:, :], x0[:, :]).then_inc(S["x0b"], 1)

            def add_x(j, k):
                n = MIXES[k]
                pool.wait_ge(S["mix"], 10 * j + 2 * k + 2)
                g.tensor_tensor(seqs(mix[n][:, :]), seqs(mix[n][:, :]), now(xn1[:, :]), ALU.add).then_inc(S["x5"], 1)

            def slot(pre, att, low, top):
                Q, A, Z, T = (n is not None for n in (pre, att, low, top))
                if Z: fold(low, "x0", 2, x0, xs1, "xs1")
                if Z: row1f(low)
                if Z: fold(low, "sq1", 1, sq1, sqs1, "sqs1")
                if T: restf(top)
                if Z: shift(low, "xn1", xn1, sx1, "sx1")
                if Z: add_x(low, 0)
                if Z: add_x(low, 1)
                if Q: duplicate(pre)
                if Q: kbdf(pre, 0)
                if Q: split_mask(pre)
                if Z: add_x(low, 2)
                if T: fold(top, "x2", 1, x2, xs2, "xs2")
                if T: fold(top, "sq2", 1, sq2, sqs2, "sqs2")
                if Q: kbdf(pre, 1)
                if Z: add_x(low, 3)
                if Z: add_x(low, 4)
                if T: shift(top, "xn2", xn2, sx2, "sx2")
                if A: fold(att, "u", 2, u, us, "us")
                if Q: kbdf(pre, 2)
                if Q: kbdf(pre, 3)
                if Z: x0bf(low)
                if A: fold(att, "sq0", 1, sq0, sqs0, "sqs0")

            weights_ready(pool)
            all_steps(pool, slot)


def kernel(**inputs):
    import numpy as np
    import concourse.bacc as bacc
    from concourse.bass_utils import run_bass_kernel_spmd

    I = {k: np.asarray(v) for k, v in inputs.items()}
    L0 = {k[9:]: v for k, v in I.items() if k.startswith("L0_xattn_")}
    L1 = {k[9:]: v for k, v in I.items() if k.startswith("L1_xattn_")}

    def cm(a):
        return a.reshape(STEPS, TOK, 2, P).transpose(0, 3, 2, 1).reshape(STEPS, P, CM)

    def rows(w):
        return w.reshape(2, P, -1).transpose(1, 0, 2).reshape(P, -1)

    def pad(w):
        return np.concatenate([w, np.zeros((P - w.shape[0], w.shape[1]), w.dtype)])

    q_order = np.arange(E).reshape(KV, 2, 2, HD).transpose(1, 2, 0, 3).reshape(-1)
    o_order = np.arange(E).reshape(KV, 2, 2, HD).transpose(2, 1, 0, 3).reshape(-1)
    ctx = I["ctx_2048"]
    first = ctx[:, 0:2, :].reshape(STEPS, NB, 2, 2, P)[:, :, ::-1].transpose(0, 4, 2, 3, 1).reshape(STEPS, P, 16)
    s0 = ctx[:, 2:2 + HS, :].reshape(STEPS, NB, 2, P, HS).transpose(0, 3, 4, 2, 1).reshape(STEPS, P, 64)

    p = np.arange(P)
    same = (p[:, None] // HS == p[None, :] // HS).astype(np.float32)
    eye = np.eye(P, dtype=np.float32)
    table = {"ident": eye, "mean256": np.full((P, P), 1.0 / E, np.float32), "sum8": same, "mean8": same / HS,
             "center8": eye - same / HS, "maskid": (p[:, None] % L == p[None, :] % L).astype(np.float32)}
    for d in range(HS):
        table[f"red{d}"] = same * ((p[None, :] % HS == d) - np.float32(1.0 / HS))
    bd = ((p[:, None] % 64) // HD == np.arange(KV)[None, :]).astype(np.float32)
    consts = np.concatenate([table[n].astype(np.float32) for n in CONST] + [bd], axis=1)

    w0 = {"wq": rows(L0["Wq"][:, q_order]), "wk": rows(np.concatenate([L0["Wk"]] * 2, 1)), "wv": rows(L0["Wv"]),
          "wo": rows(L0["Wo"][o_order]), "bv": np.repeat(L0["bv"][None], P, 0)}
    w1 = {"w1": rows(L1["maa_w1"]), "w2": L1["maa_w2"][:4].reshape(P, E), "w2b": pad(L1["maa_w2"][4]),
          "dw1": rows(L1["decay_w1"]), "dw2": pad(L1["decay_w2"]), "wr": rows(L1["Wr"].T), "wkk": rows(L1["Wk"].T),
          "wvv": rows(L1["Wv"].T), "wg": rows(L1["Wg"].T), "woo": rows(L1["Wo"].T), "fr": rows(L1["ffn_Wr"].T),
          "fk": rows(L1["ffn_Wk"].T), "fv": rows(L1["ffn_Wv"].T)}
    vecs = {"bq": L0["bq"][q_order], "bk": np.concatenate([L0["bk"]] * 4), "bo": L0["bo"], "gamma": L0["gamma"],
            "beta": L0["beta"], "ln1w": L1["ln1_w"], "ln1b": L1["ln1_b"], "ln2w": L1["ln2_w"], "ln2b": L1["ln2_b"],
            "maax": L1["maa_x"], "td": L1["time_decay"], "u": L1["faaaa"].reshape(-1), "gnw": L1["gn_w"],
            "gnb": L1["gn_b"], "fmk": L1["ffn_maa_k"], "fmr": L1["ffn_maa_r"]}
    for n in range(5):
        vecs[f"maa{n}"] = L1["maa_stack"][n]

    arrays = {
        "xT": cm(I["x"]), "cT": cm(ctx),
        "mask": I["mask_Bx1xSxS2_ff0"].reshape(STEPS, NB, L, L).transpose(0, 2, 1, 3).reshape(STEPS, L, NB * L),
        "first": first[:, :, 0:FIRST], "rest": np.concatenate([first[:, :, FIRST:], s0], axis=2),
        "consts": consts,
        "w0": np.concatenate([w0[n] for n in W0_COLS], axis=1),
        "w1": np.concatenate([w1[n] for n in W1_COLS], axis=1),
        "vec": np.concatenate([vecs[n].reshape(2, P).T for n in VEC], axis=1),
    }
    arrays = {k: np.ascontiguousarray(a) for k, a in arrays.items()}
    nc = bacc.Bacc("TRN2", target_bir_lowering=False, num_devices=1)
    args = [nc.dram_tensor(k, a.shape, F32, kind="ExternalInput").ap() for k, a in arrays.items()]
    out = nc.dram_tensor("out", (STEPS, P, CM), F32, kind="ExternalOutput").ap()
    xattn_rwkv(nc, *args, out)
    r = run_bass_kernel_spmd(nc, [arrays], core_ids=[0])
    y = r.results[0]["out"]
    return y.reshape(STEPS, P, 2, TOK).transpose(0, 3, 2, 1).reshape(B, L, E)
```
